# Optimizing a Trainium2 kernel written in Bass

```python
import numpy as np
import jax
import jax.numpy as jnp

def _softmax(x, axis=-1):
    return jax.nn.softmax(x, axis=axis)

def _gelu(x):
    return jax.nn.gelu(x, approximate=True)

def _silu(x):
    return jax.nn.silu(x)

def _sigmoid(x):
    return jax.nn.sigmoid(x)

def _layernorm(x, axis=-1, eps=1e-05):
    m = jnp.mean(x, axis=axis, keepdims=True)
    v = jnp.var(x, axis=axis, keepdims=True)
    return (x - m) / jnp.sqrt(v + eps)

def _scatter_add(tgt, idx, src, axis=0):
    return tgt.at[idx].add(src)

def _segment_sum(src, seg, n):
    return jax.ops.segment_sum(src, seg, n)
kernel_name = 'mk_gnn_preln_d1_gnn_r8_0cdbfd'

def setup_inputs(seed: int=0):
    np.random.seed(seed)
    _w = jnp.asarray

    def _rec_inputs():
        import jax
        import jax.numpy as jnp
        _gk = jax.random.key(seed)
        x = -0.0008691 + 1 * jax.random.normal(jax.random.fold_in(_gk, 1), (6250, 128), jnp.float32)
        _s = jax.random.randint(jax.random.fold_in(_gk, 2), (100000,), 0, 6250, jnp.int32)
        _d = jax.random.randint(jax.random.fold_in(_gk, 3), (100000,), 0, 6250, jnp.int32)
        _loop = jnp.arange(6250, dtype=jnp.int32)
        src = jnp.concatenate([_s, _d, _loop])
        dst = jnp.concatenate([_d, _s, _loop])
        _o = jnp.argsort(dst, stable=True)
        src = src[_o]
        dst = dst[_o]
        return (x, src, dst)
    x, src, dst = _rec_inputs()

    def _L0_gnn_setup():
        import jax, jax.numpy as jnp
        import numpy as np
        N_NODES = 1250
        N_EDGES = 80000
        IN_CH = 128
        OUT_CH = 128
        key = jax.random.key(seed)
        k1, k2, k3, k4 = jax.random.split(key, 4)
        x = jax.random.normal(k1, (N_NODES, IN_CH), dtype=jnp.float32)
        edge_index = jax.random.randint(k2, (2, N_EDGES), 0, N_NODES, dtype=jnp.int64)
        bound = 1.0 / np.sqrt(2 * IN_CH)
        W = jax.random.uniform(k3, (OUT_CH, 2 * IN_CH), dtype=jnp.float32, minval=-bound, maxval=bound)
        b = jax.random.uniform(k4, (OUT_CH,), dtype=jnp.float32, minval=-bound, maxval=bound)
        return {'x': x, 'W': W, 'b': b, 'edge_index': edge_index}
    _L0_gnn_all = _L0_gnn_setup()
    _L0_gnn_in = {k: v for k, v in _L0_gnn_all.items() if k in ('W', 'b')}
    del _L0_gnn_all
    return {'x': x, 'src': src, 'dst': dst, 'L0_gnn_W': _L0_gnn_in['W'], 'L0_gnn_b': _L0_gnn_in['b']}

def reference(x, src, dst, L0_gnn_W, L0_gnn_b):
    import jax
    import jax.numpy as jnp

    def _L0_gnn_ref(x, W, b, edge_index):
        import jax, jax.numpy as jnp
        import numpy as np
        N_NODES = 1250
        N_EDGES = 80000
        IN_CH = 128
        OUT_CH = 128
        src, dst = (edge_index[0], edge_index[1])
        x_i = x[dst]
        x_j = x[src]
        feat = jnp.concatenate([x_i, x_j - x_i], axis=-1)
        msg = feat @ W.T + b
        out = jax.ops.segment_max(msg, dst, num_segments=x.shape[0])
        return jnp.where(jnp.isfinite(out), out, 0.0)
    edge_index = jnp.stack([src, dst])
    h = jnp.maximum(_layernorm(x, axis=-1), 0.0)
    x = x + _L0_gnn_ref(h, L0_gnn_W, L0_gnn_b, edge_index)
    return x

_drawn_inputs = setup_inputs


def setup_inputs(seed=0):
    import zlib

    import numpy as np

    out = dict(_drawn_inputs(seed))
    spreads = {}
    factors = {}
    for name, (base, spread) in spreads.items():
        noise = np.random.default_rng([zlib.crc32(name.encode()), seed]).standard_normal(out[name].shape)
        drawn = base * np.exp(spread * noise) if base else spread * noise
        out[name] = jnp.asarray(drawn.astype(out[name].dtype))
    for name, factor in factors.items():
        out[name] = (out[name] * factor).astype(out[name].dtype)
    return out
```

```python
from contextlib import ExitStack

import concourse.bass as bass
from concourse import mybir

P = 128
F32 = mybir.dt.float32
BF16 = mybir.dt.bfloat16
I32 = mybir.dt.int32
ALU = mybir.AluOpType
ACT = mybir.ActivationFunctionType
AX = mybir.AxisListType

EPS = 1e-5
LOW = -3.0e38
GROUP = 7
STEPS = 12
SLOTS = 4


def edgeconv(nc, x, src, dst, W, b, out):
    nodes, D = x.shape
    edges = src.shape[0]
    tiles = -(-nodes // P)
    groups = tiles // GROUP
    full = nodes // P
    rest = nodes - full * P
    cols = -(-edges // P)
    turns = cols // (STEPS * SLOTS)
    FULL_TURN = [STEPS] * SLOTS
    left = cols - turns * STEPS * SLOTS
    LAST_TURN = [min(STEPS, left - i) for i in range(0, left, STEPS)]
    blocks_all = turns * SLOTS + len(LAST_TURN)
    steps_all = cols + blocks_all
    last_half = (blocks_all - 1) % 2
    tail = edges - (P - 1) * cols
    assert D == P and tiles % GROUP == 0 and 0 < tail <= cols and rest and tiles == full + 1
    assert turns > 2 and 0 < len(LAST_TURN) < SLOTS
    GW = GROUP * D

    near = nc.dram_tensor("near_table", (tiles * P, D), F32, kind="Internal").ap()
    running = nc.dram_tensor("running_max", (P * cols, D), F32, kind="Internal").ap()
    running_by_part = running.rearrange("(p t) d -> p t d", p=P)
    x_tiles = x[0:full * P, :].rearrange("(j p) d -> p j d", p=P)
    out_tiles = out[0:full * P, :].rearrange("(j p) d -> p j d", p=P)
    near_tiles = near.rearrange("(j p) d -> p j d", p=P)

    with ExitStack() as ctx:
        def sb(name, shape, dt):
            return ctx.enter_context(nc.sbuf_tensor(name, shape, dt))

        def sem(name):
            return ctx.enter_context(nc.semaphore(name))

        xs = sb("xs", [P, tiles, D], F32)
        hT = sb("hT", [P, tiles * P], F32)
        dense = sb("dense", [P, tiles, D], F32)
        xn = sb("xn", [P, 2, GROUP, D], F32)
        stats = sb("stats", [P, GROUP, 6], F32)
        mv = sb("mv", [P, tiles, 2], F32)
        std = sb("std", [P, tiles], F32)
        rstd = sb("rstd", [P, tiles], F32)
        w_sb = sb("w_sb", [P, 2 * D], F32)
        w_diff = sb("w_diff", [P, D], F32)
        wT = sb("wT", [P, 2, D], F32)
        bias = sb("bias", [P, D], F32)
        eps = sb("eps", [P, 1], F32)
        iota_i = sb("iota_i", [P, P], I32)
        part_i = sb("part_i", [P, 1], I32)
        iota_f = sb("iota_f", [P, P], F32)
        part_f = sb("part_f", [P, 1], F32)
        ident = sb("ident", [P, P], F32)
        step_down = sb("step_down", [P, P], F32)
        ones = sb("ones", [P, P], F32)
        last_row = sb("last_row", [P, P], F32)
        zeros_b = sb("zeros_b", [P, P], BF16)

        src_sb = sb("src_sb", [P, cols], I32)
        dst_sb = sb("dst_sb", [P, cols], I32)
        dst_f = sb("dst_f", [P, cols], F32)
        fresh = sb("fresh", [P, cols], F32)
        lo_i = sb("lo_i", [P, cols], I32)
        lo = sb("lo", [P, cols], BF16)
        hi = sb("hi", [P, cols], BF16)
        before_i = sb("before_i", [P, 2], I32)
        before = sb("before", [P, 1], F32)
        run = sb("run", [P, 1], F32)
        linked = sb("linked", [P, 1], F32)
        linked_low = sb("linked_low", [P, 1], F32)
        whole = sb("whole", [P, 1], F32)
        whole_diag = sb("whole_diag", [P, P], F32)
        whole_low = sb("whole_low", [P, P], F32)
        mend_f = sb("mend_f", [P, 1], F32)
        mend_idx = sb("mend_idx", [P, 1], I32)

        idx = sb("idx", [P, SLOTS, STEPS], I32)
        rows = sb("rows", [P, max(tiles, SLOTS * STEPS), D], F32)
        fresh_blk = sb("fresh_blk", [P, 2, STEPS], F32)
        maxima = sb("maxima", [P, 2, STEPS, D], F32)
        le = sb("le", [P, 2, STEPS, P], BF16)
        eq = sb("eq", [P, 2, STEPS, tiles], BF16)

        counts = sb("counts", [P, tiles], F32)
        ends = sb("ends", [P, tiles], F32)
        upto = sb("upto", [P, tiles], F32)
        has_edges = sb("has_edges", [P, tiles], F32)
        last_edge = sb("last_edge", [P, tiles], I32)
        tails_T = sb("tails_T", [P, P], F32)
        carried_T = sb("carried_T", [P, P + 1], F32)
        mend = sb("mend", [P, D], F32)
        mended = sb("mended", [P, D], F32)

        ps = ctx.enter_context(nc.psum_tensor("ps", [P, 8 * 512], F32))
        t_ps = [ps[:, i * 1024:i * 1024 + GW] for i in range(2)]
        m_ps = [ps[:, 2048 + i * 1024:2048 + i * 1024 + GW] for i in range(2)]

        def run_ps(h, t):
            at = (h * STEPS + t) * D
            return ps[:, at:at + D]

        iota_ps = ps[:, 6 * 512:6 * 512 + P]
        count_ps = ps[:, 7 * 512:7 * 512 + tiles]
        totals_ps = ps[:, 0:tiles]
        degree_ps = ps[:, 512:512 + tiles]
        tailT_ps = ps[:, 1024:1024 + P]
        carry_ps = ps[:, 1536:1536 + P]
        whole_ps = ps[:, 7 * 512 + 128:7 * 512 + 256]

        x_pad_set = sem("x_pad_set")
        edge_pad_set = sem("edge_pad_set")
        x_in = [sem(f"x_in{g}") for g in range(groups)]
        w_in = sem("w_in")
        bias_in = sem("bias_in")
        src_in = sem("src_in")
        dst_in = sem("dst_in")
        iota_set = sem("iota_set")
        dve_step = sem("dve_step")
        eps_set = sem("eps_set")
        ident_set = sem("ident_set")
        w_ready = sem("w_ready")
        wT_made = sem("wT_made")
        wT_ready = sem("wT_ready")
        var_ready = sem("var_ready")
        std_ready = sem("std_ready")
        rstd_ready = sem("rstd_ready")
        xn_ready = sem("xn_ready")
        xT_made = sem("xT_made")
        hT_ready = sem("hT_ready")
        near_made = sem("near_made")
        near_ready = sem("near_ready")
        near_out = sem("near_out")
        self_made = sem("self_made")
        self_ready = sem("self_ready")
        idx_in = [sem(f"idx_in{s}") for s in range(SLOTS)]
        block_begun = sem("block_begun")
        gathered = [sem(f"gathered{s}") for s in range(SLOTS)]
        chain = sem("chain")
        evacuated = sem("evacuated")
        maxima_out = [sem(f"maxima_out{h}") for h in range(2)]
        flags_ready = sem("flags_ready")
        counted = sem("counted")
        count_open = sem("count_open")
        count_done = sem("count_done")
        counts_ready = sem("counts_ready")
        totals_made = sem("totals_made")
        last_ready = sem("last_ready")
        mend_idx_ready = sem("mend_idx_ready")
        whole_ready = sem("whole_ready")
        whole_made = sem("whole_made")
        tailT_made = sem("tailT_made")
        carried_ready = sem("carried_ready")
        carry_made = sem("carry_made")
        mend_in = sem("mend_in")
        mended_ready = sem("mended_ready")
        mended_out = sem("mended_out")
        final_in = [sem(f"final_in{g}") for g in range(groups)]
        final_ready = sem("final_ready")
        out_done = sem("out_done")

        block = ctx.enter_context(nc.Block())
        CH = STEPS + 1

        @block.sync
        def _(sp):
            sp.dma_start(xs[:, 0:GROUP, :], x_tiles[:, 0:GROUP, :]).then_inc(x_in[0], 16)
            for g in range(1, groups):
                hi_tile = min(full, (g + 1) * GROUP)
                sp.dma_start(xs[:, g * GROUP:hi_tile, :], x_tiles[:, g * GROUP:hi_tile, :]).then_inc(x_in[g], 16)
            sp.wait_ge(x_pad_set, 1)
            sp.dma_start(xs[0:rest, full, :], x[full * P:nodes, :]).then_inc(x_in[groups - 1], 16)
            for g in range(groups):
                sp.wait_ge(near_ready, g + 1)
                sp.dma_start(near_tiles[:, g * GROUP:(g + 1) * GROUP, :],
                             dense[:, g * GROUP:(g + 1) * GROUP, :]).then_inc(near_out, 16)

            def indices(blk, s, n):
                sp.dma_start(idx[:, s, 0:n], src_sb[:, bass.ds(blk * STEPS, n)]).then_inc(idx_in[s], 16)

            def blocks(k, sizes, following):
                for s, n in enumerate(sizes):
                    blk = k * SLOTS + s
                    if s < len(following):
                        sp.wait_ge(chain, blk * CH + n + 1)
                        indices(blk + SLOTS, s, following[s])
                    sp.wait_ge(evacuated, blk + 1)
                    sp.dma_start(running_by_part[:, bass.ds(blk * STEPS, n), :],
                                 maxima[:, s % 2, 0:n, :]).then_inc(maxima_out[s % 2], 16)

            sp.wait_ge(src_in, 32)
            for s in range(SLOTS):
                indices(s, s, STEPS)
            with sp.Fori(0, turns - 1) as k:
                blocks(k, FULL_TURN, FULL_TURN)
            blocks(turns - 1, FULL_TURN, LAST_TURN)
            blocks(turns, LAST_TURN, [])

            for g in range(groups):
                sp.wait_ge(final_ready, g + 1)
                hi_tile = min(full, (g + 1) * GROUP)
                sp.dma_start(out_tiles[:, g * GROUP:hi_tile, :],
                             rows[:, g * GROUP:hi_tile, :]).then_inc(out_done, 16)
            sp.dma_start(out[full * P:nodes, :], rows[0:rest, full, :]).then_inc(out_done, 16)
            sp.wait_ge(out_done, 16 * (groups + 1))

        @block.scalar
        def _(act):
            act.dma_start(w_sb[:, :], W).then_inc(w_in, 16)
            act.dma_start(bias[:, :], b[None, :].to_broadcast([P, D])).then_inc(bias_in, 16)
            act.wait_ge(edge_pad_set, 3)
            act.dma_start(dst_sb[0:P - 1, :], dst[0:(P - 1) * cols].rearrange("(p t) -> p t", t=cols)).then_inc(dst_in, 16)
            act.dma_start(dst_sb[P - 1:P, 0:tail], dst[(P - 1) * cols:edges][None, :]).then_inc(dst_in, 16)
            act.dma_start(before_i[1:P, :], bass.AP(dst.tensor, dst.offset + cols - 1,
                                                    [[cols, P - 1], [1, 2]])).then_inc(dst_in, 16)
            act.dma_start(src_sb[0:P - 1, :], src[0:(P - 1) * cols].rearrange("(p t) -> p t", t=cols)).then_inc(src_in, 16)
            act.dma_start(src_sb[P - 1:P, 0:tail], src[(P - 1) * cols:edges][None, :]).then_inc(src_in, 16)

            act.wait_ge(wT_made, 1)
            nc.scalar.copy(wT[:, :, :].rearrange("p a d -> p (a d)"), t_ps[0][:, 0:2 * D]).then_inc(wT_ready, 1)

            def deviations(g):
                act.wait_ge(var_ready, g + 1)
                if g == 0:
                    act.wait_ge(eps_set, 1)
                at = slice(g * GROUP, (g + 1) * GROUP)
                nc.scalar.activation(std[:, at], mv[:, at, 1], ACT.Sqrt, bias=eps[:, 0:1]).then_inc(std_ready, 1)

            def relu(g):
                act.wait_ge(xT_made, g + 1)
                nc.scalar.activation(hT[:, g * GW:(g + 1) * GW], t_ps[g % 2], ACT.Relu).then_inc(hT_ready, 1)

            deviations(0)
            for g in range(1, groups):
                deviations(g)
                relu(g - 1)
            relu(groups - 1)

            def blocks(k, first, sizes):
                for s, n in enumerate(sizes):
                    blk = k * SLOTS + s
                    h = s % 2
                    if not (first and s < 2):
                        act.wait_ge(maxima_out[h], (k * (SLOTS // 2) + s // 2) * 16)
                    act.wait_ge(chain, blk * CH + n + 1)
                    half = ps[:, h * STEPS * D:(h * STEPS + n) * D]
                    nc.scalar.copy(maxima[:, h, 0:n, :].rearrange("p t d -> p (t d)"), half).then_inc(evacuated, 1)

            blocks(0, True, FULL_TURN)
            with act.Fori(1, turns) as k:
                blocks(k, False, FULL_TURN)
            blocks(turns, False, LAST_TURN)

        @block.gpsimd
        def _(pool):
            nc.gpsimd.memset(xs[:, full, :], 0.0).then_inc(x_pad_set, 1)
            nc.gpsimd.memset(dst_sb[:, tail:cols], 64 * P - 1).then_inc(edge_pad_set, 1)
            nc.gpsimd.memset(src_sb[:, tail:cols], 0).then_inc(edge_pad_set, 1)
            nc.gpsimd.memset(before_i[:, :], -1).then_inc(edge_pad_set, 1)
            nc.gpsimd.iota(iota_i[:, :], [[1, P]], base=0, channel_multiplier=0).then_inc(iota_set, 1)
            nc.gpsimd.iota(part_i[:, :], [[0, 1]], base=0, channel_multiplier=1).then_inc(iota_set, 1)
            for g in range(groups):
                pool.wait_ge(rstd_ready, g + 1)
                if g >= 2:
                    pool.wait_ge(xT_made, g - 1)
                for i in range(GROUP):
                    j = g * GROUP + i
                    last = nc.gpsimd.tensor_scalar(xn[:, g % 2, i, :], xs[:, j, :], mv[:, j, 0:1], rstd[:, j:j + 1],
                                                   ALU.subtract, ALU.mult)
                last.then_inc(xn_ready, 1)

            pool.wait_ge(near_out, 16 * groups)

            def blocks(k, sizes):
                for s, n in enumerate(sizes):
                    pool.wait_ge(idx_in[s], k * 16 + 16)
                    pool.sem_inc(block_begun, 1)
                    for t in range(n):
                        nc.gpsimd.indirect_dma_start(
                            rows[:, s * STEPS + t, :], None, near[:, :],
                            bass.IndirectOffsetOnAxis(idx[:, s, t:t + 1], 0)).then_inc(gathered[s], 16)

            with pool.Fori(0, turns) as k:
                blocks(k, FULL_TURN)
            blocks(turns, LAST_TURN)

            pool.wait_ge(mend_idx_ready, 1)
            for h in range(2):
                pool.wait_ge(maxima_out[h], (blocks_all + 1 - h) // 2 * 16)
            nc.gpsimd.indirect_dma_start(mend[:, :], None, running[:, :],
                                         bass.IndirectOffsetOnAxis(mend_idx[:, 0:1], 0)).then_inc(mend_in, 16)
            pool.wait_ge(mended_ready, 1)
            nc.gpsimd.indirect_dma_start(running[:, :], bass.IndirectOffsetOnAxis(mend_idx[:, 0:1], 0),
                                         mended[:, :], None).then_inc(mended_out, 16)
            pool.wait_ge(last_ready, 1)
            pool.wait_ge(chain, steps_all)
            pool.wait_ge(mended_out, 16)
            for j in range(tiles):
                nc.gpsimd.indirect_dma_start(
                    rows[:, j, :], None, running[:, :],
                    bass.IndirectOffsetOnAxis(last_edge[:, j:j + 1], 0)).then_inc(final_in[j // GROUP], 16)

        @block.tensor
        def _(pe):
            pe.wait_ge(ident_set, 1)
            pe.wait_ge(w_ready, 1)
            nc.tensor.transpose(t_ps[0][:, 0:D], w_sb[:, D:2 * D], ident[:, :])
            nc.tensor.transpose(t_ps[0][:, D:2 * D], w_diff[:, :], ident[:, :]).then_inc(wT_made, 1)

            def transposes(g):
                pe.wait_ge(xn_ready, g + 1)
                if g == 0:
                    pe.wait_ge(wT_ready, 1)
                if g >= 2:
                    pe.wait_ge(hT_ready, g - 1)
                for i in range(GROUP):
                    last = nc.tensor.transpose(t_ps[g % 2][:, i * D:(i + 1) * D], xn[:, g % 2, i, :], ident[:, :])
                last.then_inc(xT_made, 1)

            def products(g, which, made, turn):
                for i in range(GROUP):
                    j = g * GROUP + i
                    last = nc.tensor.matmul(m_ps[turn % 2][:, i * D:(i + 1) * D], hT[:, j * P:(j + 1) * P],
                                            wT[:, which, :], start=True, stop=True)
                last.then_inc(made, 1)

            def near_products(g):
                pe.wait_ge(hT_ready, g + 1)
                if g >= 2:
                    pe.wait_ge(near_ready, g - 1)
                products(g, 0, near_made, g)

            transposes(0)
            for g in range(1, groups):
                transposes(g)
                near_products(g - 1)
            near_products(groups - 1)
            for g in range(groups):
                turn = groups + g
                if g < 2:
                    pe.wait_ge(near_ready, turn - 1)
                else:
                    pe.wait_ge(self_ready, g - 1)
                products(g, 1, self_made, turn)

            pe.wait_ge(self_ready, groups)
            nc.tensor.matmul(count_ps, zeros_b[:, :], zeros_b[:, 0:tiles], start=True, stop=False,
                             skip_group_check=True).then_inc(count_open, 1)

            def blocks(k, sizes):
                for s, n in enumerate(sizes):
                    pe.wait_ge(flags_ready, k * SLOTS + (s + 1))
                    for t in range(n):
                        last = nc.tensor.matmul(count_ps, le[:, s % 2, t, :], eq[:, s % 2, t, :], start=False,
                                                stop=False, skip_group_check=True)
                    last.then_inc(counted, 1)

            pe.wait_ge(count_open, 1)
            with pe.Fori(0, turns) as k:
                blocks(k, FULL_TURN)
            blocks(turns, LAST_TURN)
            pe.wait_ge(counted, blocks_all)
            nc.tensor.matmul(count_ps, zeros_b[:, :], zeros_b[:, 0:tiles], start=False, stop=True,
                             skip_group_check=True).then_inc(count_done, 1)
            pe.wait_ge(evacuated, blocks_all)
            nc.tensor.transpose(tailT_ps, maxima[:, last_half, LAST_TURN[-1] - 1, :], ident[:, :]).then_inc(tailT_made, 1)
            pe.wait_ge(whole_ready, 1)
            nc.tensor.matmul(whole_ps, ones[:, :], whole_diag[:, :], start=True, stop=True).then_inc(whole_made, 1)
            pe.wait_ge(counts_ready, 1)
            nc.tensor.matmul(totals_ps, last_row[:, :], counts[:, :], start=True, stop=True)
            nc.tensor.matmul(degree_ps, step_down[:, :], counts[:, :], start=True, stop=True).then_inc(totals_made, 1)
            pe.wait_ge(carried_ready, 1)
            nc.tensor.transpose(carry_ps, carried_T[:, 0:P], ident[:, :]).then_inc(carry_made, 1)

        @block.vector
        def _(dve):
            own = [0]

            def then(ins):
                own[0] += 1
                ins.then_inc(dve_step, 1)

            def settled():
                dve.wait_ge(dve_step, own[0])

            nc.vector.memset(eps[:, :], EPS).then_inc(eps_set, 1)
            then(nc.vector.memset(ones[:, :], 1.0))
            dve.wait_ge(iota_set, 2)
            then(nc.vector.tensor_copy(iota_f[:, :], iota_i[:, :]))
            then(nc.vector.tensor_copy(part_f[:, :], part_i[:, :]))
            settled()
            then(nc.vector.tensor_scalar(ident[:, :], iota_f[:, :], part_f[:, 0:1], None, ALU.is_equal))
            settled()
            nc.vector.memset(zeros_b[:, :], 0.0).then_inc(ident_set, 1)
            dve.wait_ge(w_in, 16)
            nc.vector.tensor_tensor(w_diff[:, :], w_sb[:, 0:D], w_sb[:, D:2 * D], ALU.subtract).then_inc(w_ready, 1)

            def statistics(g):
                dve.wait_ge(x_in[g], 32 if g == groups - 1 else 16)
                for i in range(GROUP):
                    then(nc.vector.bn_stats(stats[:, i, :], xs[:, g * GROUP + i, :]))
                settled()
                for i in range(GROUP):
                    last = nc.vector.bn_aggr(mv[:, g * GROUP + i, :], stats[:, i, :])
                last.then_inc(var_ready, 1)

            def reciprocals(g):
                dve.wait_ge(std_ready, g + 1)
                at = slice(g * GROUP, (g + 1) * GROUP)
                nc.vector.reciprocal(rstd[:, at], std[:, at]).then_inc(rstd_ready, 1)

            def near_copy(g):
                dve.wait_ge(near_made, g + 1)
                nc.vector.tensor_copy(dense[:, g * GROUP:(g + 1) * GROUP, :].rearrange("p j d -> p (j d)"),
                                      m_ps[g % 2]).then_inc(near_ready, 1)

            statistics(0)
            reciprocals(0)
            statistics(1)
            reciprocals(1)
            for g in range(2, groups):
                statistics(g)
                reciprocals(g)
                near_copy(g - 2)
            near_copy(groups - 2)
            near_copy(groups - 1)

            dve.wait_ge(bias_in, 16)
            dve.wait_ge(near_out, 16 * groups)
            for g in range(groups):
                dve.wait_ge(self_made, g + 1)
                nc.vector.tensor_tensor(dense[:, g * GROUP:(g + 1) * GROUP, :],
                                        m_ps[(groups + g) % 2].rearrange("p (j d) -> p j d", d=D),
                                        bias[:, None, :].to_broadcast([P, GROUP, D]), ALU.add).then_inc(self_ready, 1)

            dve.wait_ge(dst_in, 48)
            then(nc.vector.tensor_copy(dst_f[:, :], dst_sb[:, :]))
            settled()
            then(nc.vector.tensor_tensor(fresh[:, 1:cols], dst_f[:, 1:cols], dst_f[:, 0:cols - 1], ALU.not_equal))
            then(nc.vector.memset(fresh[:, 0:1], 1.0))
            settled()
            then(nc.vector.tensor_scalar(fresh[:, :], fresh[:, :], LOW, None, ALU.mult))
            then(nc.vector.tensor_scalar(lo_i[:, :], dst_sb[:, :], P - 1, None, ALU.bitwise_and))
            settled()
            then(nc.vector.tensor_copy(lo[:, :], lo_i[:, :]))
            settled()
            then(nc.vector.tensor_scalar(lo_i[:, :], dst_sb[:, :], P.bit_length() - 1, None, ALU.logical_shift_right))
            settled()
            then(nc.vector.tensor_copy(hi[:, :], lo_i[:, :]))
            dve.wait_ge(self_ready, groups)
            then(nc.vector.tensor_copy(iota_ps, iota_f[:, :]))
            then(nc.vector.memset(run_ps(1, STEPS - 1), LOW))
            settled()

            def blocks(k, first, sizes):
                for s, n in enumerate(sizes):
                    blk = k * SLOTS + s
                    h = s % 2
                    base = blk * CH
                    if not (first and s == 0):
                        dve.wait_ge(chain, base)
                    nc.vector.tensor_scalar(fresh_blk[:, h, 0:n], fresh[:, bass.ds(blk * STEPS, n)], 0.0, None,
                                            ALU.add).then_inc(chain, 1)
                    if not (first and s == 0):
                        dve.wait_ge(evacuated, blk)
                    dve.wait_ge(gathered[s], k * (16 * STEPS) + 16 * n)
                    for t in range(n):
                        before_ps = run_ps(h, t - 1) if t else run_ps(1 - h, STEPS - 1)
                        dve.wait_ge(chain, base + (t + 1))
                        nc.vector.scalar_tensor_tensor(run_ps(h, t), before_ps, fresh_blk[:, h, t:t + 1],
                                                       rows[:, s * STEPS + t, :], ALU.add, ALU.max).then_inc(chain, 1)
                    if not (first and s < 2):
                        dve.wait_ge(counted, blk - 1)
                    at = bass.ds(blk * STEPS, n)
                    nc.vector.tensor_tensor(le[:, h, 0:n, :], iota_ps[:, None, :].to_broadcast([P, n, P]),
                                            lo[:, at, None].to_broadcast([P, n, P]), ALU.is_ge)
                    nc.vector.tensor_tensor(eq[:, h, 0:n, :], iota_ps[:, None, 0:tiles].to_broadcast([P, n, tiles]),
                                            hi[:, at, None].to_broadcast([P, n, tiles]),
                                            ALU.is_equal).then_inc(flags_ready, 1)

            then(nc.vector.tensor_copy(before[:, :], before_i[:, 0:1]))
            then(nc.vector.tensor_scalar(lo_i[:, :], dst_f[:, :], dst_f[:, 0:1], None, ALU.is_equal))
            settled()
            then(nc.vector.reduce_sum(run[:, :], lo_i[:, :], AX.X))
            then(nc.vector.tensor_tensor(linked[:, :], before[:, :], dst_f[:, 0:1], ALU.is_equal))
            settled()
            then(nc.vector.tensor_scalar(linked_low[:, :], linked[:, :], 1.0, -LOW, ALU.subtract, ALU.mult))
            then(nc.vector.scalar_tensor_tensor(whole[:, :], run[:, :], float(cols), linked[:, :], ALU.is_equal, ALU.mult))
            then(nc.vector.tensor_scalar(mend_f[:, :], part_f[:, :], float(cols), -1.0, ALU.mult, ALU.add))
            settled()
            nc.vector.tensor_scalar(whole_diag[:, :], ident[:, :], whole[:, 0:1], None, ALU.mult).then_inc(whole_ready, 1)
            nc.vector.tensor_tensor(mend_idx[:, :], mend_f[:, :], run[:, :], ALU.add).then_inc(mend_idx_ready, 1)
            then(nc.vector.tensor_scalar(step_down[:, :], iota_f[:, :], part_f[:, 0:1], 1.0, ALU.subtract, ALU.is_equal))
            then(nc.vector.tensor_scalar(whole_low[:, 0:1], part_f[:, :], float(P - 1), None, ALU.is_equal))
            settled()
            then(nc.vector.tensor_tensor(step_down[:, :], ident[:, :], step_down[:, :], ALU.subtract))
            then(nc.vector.tensor_scalar(last_row[:, :], ones[:, :], whole_low[:, 0:1], None, ALU.mult))
            settled()

            blocks(0, True, FULL_TURN)
            with dve.Fori(1, turns) as k:
                blocks(k, False, FULL_TURN)
            blocks(turns, False, LAST_TURN)

            dve.wait_ge(whole_made, 1)
            then(nc.vector.tensor_scalar(whole_low[:, :], whole_ps, 1.0, -LOW, ALU.subtract, ALU.mult))
            dve.wait_ge(tailT_made, 1)
            then(nc.vector.tensor_copy(tails_T[:, :], tailT_ps))
            then(nc.vector.memset(carried_T[:, 0:1], 0.0))
            settled()
            nc.vector.tensor_tensor_scan(carried_T[:, 1:P + 1], whole_low[:, :], tails_T[:, :], LOW,
                                         ALU.add, ALU.max).then_inc(carried_ready, 1)
            dve.wait_ge(count_done, 1)
            nc.vector.tensor_copy(counts[:, :], count_ps).then_inc(counts_ready, 1)
            dve.wait_ge(mend_in, 16)
            dve.wait_ge(carry_made, 1)
            nc.vector.scalar_tensor_tensor(mended[:, :], carry_ps, linked_low[:, 0:1], mend[:, :],
                                           ALU.add, ALU.max).then_inc(mended_ready, 1)
            dve.wait_ge(totals_made, 1)
            then(nc.vector.tensor_copy(ends[:, :], totals_ps))
            then(nc.vector.tensor_scalar(has_edges[:, :], degree_ps, 0.0, None, ALU.is_gt))
            settled()
            then(nc.vector.tensor_tensor_scan(upto[:, :], ones[:, 0:tiles], ends[:, :], 0.0, ALU.mult, ALU.add))
            settled()
            then(nc.vector.tensor_tensor(upto[:, :], upto[:, :], ends[:, :], ALU.subtract))
            settled()
            then(nc.vector.tensor_tensor(upto[:, :], upto[:, :], counts[:, :], ALU.add))
            settled()
            nc.vector.tensor_scalar(last_edge[:, :], upto[:, :], -1.0, 0.0, ALU.add, ALU.max).then_inc(last_ready, 1)

            for g in range(groups):
                at = slice(g * GROUP, (g + 1) * GROUP)
                dve.wait_ge(final_in[g], 16 * GROUP)
                then(nc.vector.tensor_tensor(rows[:, at, :], rows[:, at, :], dense[:, at, :], ALU.add))
                settled()
                then(nc.vector.tensor_tensor(rows[:, at, :], rows[:, at, :],
                                             has_edges[:, at, None].to_broadcast([P, GROUP, D]), ALU.mult))
                settled()
                nc.vector.tensor_tensor(rows[:, at, :], rows[:, at, :], xs[:, at, :],
                                        ALU.add).then_inc(final_ready, 1)


def kernel(**inputs):
    import numpy as np
    import concourse.bacc as bacc
    from concourse.bass_utils import run_bass_kernel_spmd as run

    nc = bacc.Bacc("TRN2", target_bir_lowering=False, num_devices=1)
    arrays, args = {}, []
    for name in ["x", "src", "dst", "L0_gnn_W", "L0_gnn_b"]:
        a = np.ascontiguousarray(inputs[name])
        arrays[f"in_{name}"] = a
        args.append(nc.dram_tensor(f"in_{name}", a.shape, mybir.dt.from_np(a.dtype), kind="ExternalInput").ap())
    args.append(nc.dram_tensor("out_x", inputs["x"].shape, F32, kind="ExternalOutput").ap())
    edgeconv(nc, *args)
    return run(nc, [arrays], core_ids=[0]).results[0]["out_x"]
```

```python
from contextlib import ExitStack

import concourse.bass as bass
from concourse import mybir

P = 128
F32 = mybir.dt.float32
BF16 = mybir.dt.bfloat16
I32 = mybir.dt.int32
ALU = mybir.AluOpType
ACT = mybir.ActivationFunctionType
AX = mybir.AxisListType

EPS = 1e-5
LOW = -3.0e38
GROUP = 8
STEPS = 12
SLOTS = 4


def edgeconv(nc, x, src, dst, W, b, out):
    nodes, D = x.shape
    edges = src.shape[0]
    tiles = -(-nodes // P)
    sizes = [4] + [GROUP] * ((tiles - 4 - 5) // GROUP)
    sizes += [tiles - sum(sizes) - 2, 2] if tiles - sum(sizes) > 2 else [tiles - sum(sizes)]
    spans = [(sum(sizes[:g]), sum(sizes[:g + 1])) for g in range(len(sizes))]
    groups = len(spans)
    full = nodes // P
    rest = nodes - full * P
    cols = -(-edges // P)
    turns = cols // (STEPS * SLOTS)
    FULL_TURN = [STEPS] * SLOTS
    left = cols - turns * STEPS * SLOTS
    LAST_TURN = [min(STEPS, left - i) for i in range(0, left, STEPS)]
    blocks_all = turns * SLOTS + len(LAST_TURN)
    steps_all = cols + blocks_all
    last_half = (blocks_all - 1) % 2
    tail = edges - (P - 1) * cols
    assert D == P and max(sizes) <= GROUP and 0 < tail <= cols and rest and tiles == full + 1
    assert turns > 2 and 0 < len(LAST_TURN) < SLOTS

    near = nc.dram_tensor("near_table", (tiles * P, D), F32, kind="Internal").ap()
    running = nc.dram_tensor("running_max", (P * cols + 1, D), F32, kind="Internal").ap()
    zero_row = P * cols
    running_by_part = running[0:P * cols, :].rearrange("(p t) d -> p t d", p=P)
    x_tiles = x[0:full * P, :].rearrange("(j p) d -> p j d", p=P)
    out_tiles = out[0:full * P, :].rearrange("(j p) d -> p j d", p=P)
    near_tiles = near.rearrange("(j p) d -> p j d", p=P)

    with ExitStack() as ctx:
        def sb(name, shape, dt):
            return ctx.enter_context(nc.sbuf_tensor(name, shape, dt))

        def sem(name):
            return ctx.enter_context(nc.semaphore(name))

        xs = sb("xs", [P, tiles, D], F32)
        hT = sb("hT", [P, tiles * P], F32)
        dense = sb("dense", [P, tiles, D], F32)
        xn = sb("xn", [P, 2, GROUP, D], F32)
        stats = sb("stats", [P, 2, GROUP, 6], F32)
        mv = sb("mv", [P, tiles, 2], F32)
        std = sb("std", [P, tiles], F32)
        rstd = sb("rstd", [P, tiles], F32)
        shift = sb("shift", [P, tiles], F32)
        w_sb = sb("w_sb", [P, 2 * D], F32)
        w_diff = sb("w_diff", [P, D], F32)
        wT = sb("wT", [P, 2, D], F32)
        bias = sb("bias", [P, D], F32)
        eps = sb("eps", [P, 1], F32)
        iota_i = sb("iota_i", [P, P], I32)
        part_i = sb("part_i", [P, 1], I32)
        iota_f = sb("iota_f", [P, P], F32)
        part_f = sb("part_f", [P, 1], F32)
        ident = sb("ident", [P, P], F32)
        step_down = sb("step_down", [P, P], F32)
        ones = sb("ones", [P, P], F32)
        last_row = sb("last_row", [P, P], F32)
        zero_f = sb("zero_f", [1, D], F32)
        zeros_b = sb("zeros_b", [P, P], BF16)

        src_sb = sb("src_sb", [P, cols], I32)
        dst_sb = sb("dst_sb", [P, cols], I32)
        dst_f = sb("dst_f", [P, cols], F32)
        fresh = sb("fresh", [P, cols], F32)
        lo_i = sb("lo_i", [P, cols], I32)
        lo = sb("lo", [P, cols], BF16)
        hi = sb("hi", [P, cols], BF16)
        before_i = sb("before_i", [P, 2], I32)
        before = sb("before", [P, 1], F32)
        run = sb("run", [P, 1], F32)
        linked = sb("linked", [P, 1], F32)
        linked_low = sb("linked_low", [P, 1], F32)
        whole = sb("whole", [P, 1], F32)
        whole_diag = sb("whole_diag", [P, P], F32)
        whole_low = sb("whole_low", [P, P], F32)
        mend_f = sb("mend_f", [P, 1], F32)
        mend_idx = sb("mend_idx", [P, 1], I32)

        idx = sb("idx", [P, SLOTS, STEPS], I32)
        rows = sb("rows", [P, max(tiles, SLOTS * STEPS), D], F32)
        fresh_blk = sb("fresh_blk", [P, 2, STEPS], F32)
        maxima = sb("maxima", [P, 2, STEPS, D], F32)
        le = sb("le", [P, 2, STEPS, P], BF16)
        eq = sb("eq", [P, 2, STEPS, tiles], BF16)

        counts = sb("counts", [P, tiles], F32)
        ends = sb("ends", [P, tiles], F32)
        upto = sb("upto", [P, tiles], F32)
        has_edges = sb("has_edges", [P, tiles], F32)
        last_f = sb("last_f", [P, tiles], F32)
        last_edge = sb("last_edge", [P, tiles], I32)
        tails_T = sb("tails_T", [P, P], F32)
        carried_T = sb("carried_T", [P, P + 1], F32)
        mend = sb("mend", [P, D], F32)
        mended = sb("mended", [P, D], F32)

        ps = ctx.enter_context(nc.psum_tensor("ps", [P, 8 * 512], F32))
        t_ps = [ps[:, i * 1024:(i + 1) * 1024] for i in range(2)]
        m_ps = [ps[:, 2048 + i * 1024:2048 + (i + 1) * 1024] for i in range(2)]

        def run_ps(h, t):
            at = (h * STEPS + t) * D
            return ps[:, at:at + D]

        iota_ps = ps[:, 6 * 512:6 * 512 + P]
        count_ps = ps[:, 7 * 512:7 * 512 + tiles]
        totals_ps = ps[:, 0:tiles]
        degree_ps = ps[:, 512:512 + tiles]
        tailT_ps = ps[:, 1024:1024 + P]
        carry_ps = ps[:, 1536:1536 + P]
        whole_ps = ps[:, 7 * 512 + 128:7 * 512 + 256]

        x_pad_set = sem("x_pad_set")
        edge_pad_set = sem("edge_pad_set")
        x_in = [sem(f"x_in{g}") for g in range(groups)]
        w_in = sem("w_in")
        bias_in = sem("bias_in")
        src_in = sem("src_in")
        dst_in = sem("dst_in")
        iota_set = sem("iota_set")
        dve_step = sem("dve_step")
        eps_set = sem("eps_set")
        ident_set = sem("ident_set")
        w_ready = sem("w_ready")
        wT_made = sem("wT_made")
        wT_ready = sem("wT_ready")
        var_ready = sem("var_ready")
        std_ready = sem("std_ready")
        rstd_ready = sem("rstd_ready")
        xn_pool = sem("xn_pool")
        xn_act = sem("xn_act")
        xn_dve = sem("xn_dve")
        xT_made = sem("xT_made")
        hT_ready = sem("hT_ready")
        near_made = sem("near_made")
        near_ready = sem("near_ready")
        near_out = sem("near_out")
        self_made = sem("self_made")
        self_ready = sem("self_ready")
        idx_in = [sem(f"idx_in{s}") for s in range(SLOTS)]
        block_begun = sem("block_begun")
        gathered = [sem(f"gathered{s}") for s in range(SLOTS)]
        chain = sem("chain")
        evacuated = sem("evacuated")
        maxima_out = [sem(f"maxima_out{h}") for h in range(2)]
        flags_ready = sem("flags_ready")
        counted = sem("counted")
        count_open = sem("count_open")
        count_done = sem("count_done")
        counts_ready = sem("counts_ready")
        totals_made = sem("totals_made")
        last_ready = sem("last_ready")
        mend_idx_ready = sem("mend_idx_ready")
        whole_ready = sem("whole_ready")
        whole_made = sem("whole_made")
        tailT_made = sem("tailT_made")
        carried_ready = sem("carried_ready")
        carry_made = sem("carry_made")
        mend_in = sem("mend_in")
        mended_ready = sem("mended_ready")
        mended_out = sem("mended_out")
        zero_set = sem("zero_set")
        zero_out = sem("zero_out")
        final_in = [sem(f"final_in{g}") for g in range(groups)]
        final_ready = sem("final_ready")
        out_done = sem("out_done")

        block = ctx.enter_context(nc.Block())
        CH = STEPS + 1

        def shares(g):
            a, z = spans[g]
            p = a + (z - a) // 4
            v = p + max(1, (z - a) // 3)
            return range(a, p), range(p, v), range(v, z)


        @block.sync
        def _(sp):
            sp.dma_start(xs[:, 0:spans[0][1], :], x_tiles[:, 0:spans[0][1], :]).then_inc(x_in[0], 16)
            for g in range(1, groups):
                a, z = spans[g]
                z = min(full, z)
                sp.dma_start(xs[:, a:z, :], x_tiles[:, a:z, :]).then_inc(x_in[g], 16)
            sp.wait_ge(x_pad_set, 1)
            sp.dma_start(xs[0:rest, full, :], x[full * P:nodes, :]).then_inc(x_in[groups - 1], 16)
            sp.wait_ge(edge_pad_set, 3)
            by_part = (P - 1) * cols
            sp.dma_start(src_sb[0:P - 1, :], src[0:by_part].rearrange("(p t) -> p t", t=cols)).then_inc(src_in, 16)
            sp.dma_start(src_sb[P - 1:P, 0:tail], src[by_part:edges][None, :]).then_inc(src_in, 16)
            sp.dma_start(dst_sb[0:P - 1, :], dst[0:by_part].rearrange("(p t) -> p t", t=cols)).then_inc(dst_in, 16)
            sp.dma_start(dst_sb[P - 1:P, 0:tail], dst[by_part:edges][None, :]).then_inc(dst_in, 16)
            sp.dma_start(before_i[1:P, :], bass.AP(dst.tensor, dst.offset + cols - 1,
                                                   [[cols, P - 1], [1, 2]])).then_inc(dst_in, 16)

            def indices(blk, s, n):
                sp.dma_start(idx[:, s, 0:n], src_sb[:, bass.ds(blk * STEPS, n)]).then_inc(idx_in[s], 16)

            def blocks(k, sizes, following):
                for s, n in enumerate(sizes):
                    blk = k * SLOTS + s
                    if s < len(following):
                        sp.wait_ge(chain, blk * CH + n + 1)
                        indices(blk + SLOTS, s, following[s])
                    sp.wait_ge(evacuated, blk + 1)
                    sp.dma_start(running_by_part[:, bass.ds(blk * STEPS, n), :],
                                 maxima[:, s % 2, 0:n, :]).then_inc(maxima_out[s % 2], 16)

            for g, (a, z) in enumerate(spans):
                if g == groups // 2:
                    sp.wait_ge(src_in, 32)
                    for s in range(SLOTS):
                        indices(s, s, STEPS)
                sp.wait_ge(near_ready, g + 1)
                sp.dma_start(near_tiles[:, a:z, :], dense[:, a:z, :]).then_inc(near_out, 16)
            sp.wait_ge(zero_set, 1)
            sp.dma_start(running[zero_row:zero_row + 1, :], zero_f[:, :]).then_inc(zero_out, 16)
            with sp.Fori(0, turns - 1) as k:
                blocks(k, FULL_TURN, FULL_TURN)
            blocks(turns - 1, FULL_TURN, LAST_TURN)
            blocks(turns, LAST_TURN, [])

            for g, (a, z) in enumerate(spans):
                sp.wait_ge(final_ready, g + 1)
                z = min(full, z)
                sp.dma_start(out_tiles[:, a:z, :], rows[:, a:z, :]).then_inc(out_done, 16)
            sp.dma_start(out[full * P:nodes, :], rows[0:rest, full, :]).then_inc(out_done, 16)
            sp.wait_ge(out_done, 16 * (groups + 1))

        @block.scalar
        def _(act):
            act.dma_start(w_sb[:, :], W).then_inc(w_in, 16)
            act.dma_start(bias[:, :], b[None, :].to_broadcast([P, D])).then_inc(bias_in, 16)

            act.wait_ge(wT_made, 1)
            nc.scalar.copy(wT[:, :, :].rearrange("p a d -> p (a d)"), t_ps[0][:, 0:2 * D]).then_inc(wT_ready, 1)

            def deviations(g):
                act.wait_ge(var_ready, g + 1)
                if g == 0:
                    act.wait_ge(eps_set, 1)
                at = slice(*spans[g])
                nc.scalar.activation(std[:, at], mv[:, at, 1], ACT.Sqrt, bias=eps[:, 0:1]).then_inc(std_ready, 1)

            def normalise(g):
                act.wait_ge(rstd_ready, g + 1)
                if g >= 2:
                    act.wait_ge(xT_made, g - 1)
                for j in shares(g)[2]:
                    last = nc.scalar.activation(xn[:, g % 2, j - spans[g][0], :], xs[:, j, :], ACT.Identity,
                                                bias=shift[:, j:j + 1], scale=rstd[:, j:j + 1])
                last.then_inc(xn_act, 1)

            def relu(g):
                a, z = spans[g]
                act.wait_ge(xT_made, g + 1)
                nc.scalar.activation(hT[:, a * P:z * P], t_ps[g % 2][:, 0:(z - a) * P], ACT.Relu).then_inc(hT_ready, 1)

            def near_copy(g):
                a, z = spans[g]
                act.wait_ge(near_made, g + 1)
                nc.scalar.copy(dense[:, a:z, :].rearrange("p j d -> p (j d)"),
                               m_ps[g % 2][:, 0:(z - a) * D]).then_inc(near_ready, 1)

            for g in range(groups + 2):
                if g < groups:
                    deviations(g)
                if 1 <= g <= groups:
                    relu(g - 1)
                if g < groups:
                    normalise(g)
                if g >= 2:
                    near_copy(g - 2)

            def blocks(k, first, sizes):
                for s, n in enumerate(sizes):
                    blk = k * SLOTS + s
                    h = s % 2
                    if not (first and s < 2):
                        act.wait_ge(maxima_out[h], (k * (SLOTS // 2) + s // 2) * 16)
                    act.wait_ge(chain, blk * CH + n + 1)
                    half = ps[:, h * STEPS * D:(h * STEPS + n) * D]
                    nc.scalar.copy(maxima[:, h, 0:n, :].rearrange("p t d -> p (t d)"), half).then_inc(evacuated, 1)

            blocks(0, True, FULL_TURN)
            with act.Fori(1, turns) as k:
                blocks(k, False, FULL_TURN)
            blocks(turns, False, LAST_TURN)

        @block.gpsimd
        def _(pool):
            nc.gpsimd.memset(xs[:, full, :], 0.0).then_inc(x_pad_set, 1)
            nc.gpsimd.memset(dst_sb[:, tail:cols], 64 * P - 1).then_inc(edge_pad_set, 1)
            nc.gpsimd.memset(src_sb[:, tail:cols], 0).then_inc(edge_pad_set, 1)
            nc.gpsimd.memset(before_i[:, :], -1).then_inc(edge_pad_set, 1)
            nc.gpsimd.iota(iota_i[:, :], [[1, P]], base=0, channel_multiplier=0).then_inc(iota_set, 1)
            nc.gpsimd.iota(part_i[:, :], [[0, 1]], base=0, channel_multiplier=1).then_inc(iota_set, 1)
            for g in range(groups):
                if len(shares(g)[0]):
                    pool.wait_ge(rstd_ready, g + 1)
                    if g >= 2:
                        pool.wait_ge(xT_made, g - 1)
                    for j in shares(g)[0]:
                        last = nc.gpsimd.tensor_scalar(xn[:, g % 2, j - spans[g][0], :], xs[:, j, :], mv[:, j, 0:1],
                                                       rstd[:, j:j + 1], ALU.subtract, ALU.mult)
                    last.then_inc(xn_pool, 1)

            pool.wait_ge(near_out, 16 * groups)

            def blocks(k, sizes):
                for s, n in enumerate(sizes):
                    pool.wait_ge(idx_in[s], k * 16 + 16)
                    pool.sem_inc(block_begun, 1)
                    for t in range(n):
                        nc.gpsimd.indirect_dma_start(
                            rows[:, s * STEPS + t, :], None, near[:, :],
                            bass.IndirectOffsetOnAxis(idx[:, s, t:t + 1], 0)).then_inc(gathered[s], 16)

            with pool.Fori(0, turns) as k:
                blocks(k, FULL_TURN)
            blocks(turns, LAST_TURN)

            pool.wait_ge(mend_idx_ready, 1)
            for h in range(2):
                pool.wait_ge(maxima_out[h], (blocks_all + 1 - h) // 2 * 16)
            nc.gpsimd.indirect_dma_start(mend[:, :], None, running[:, :],
                                         bass.IndirectOffsetOnAxis(mend_idx[:, 0:1], 0)).then_inc(mend_in, 16)
            pool.wait_ge(mended_ready, 1)
            nc.gpsimd.indirect_dma_start(running[:, :], bass.IndirectOffsetOnAxis(mend_idx[:, 0:1], 0),
                                         mended[:, :], None).then_inc(mended_out, 16)
            pool.wait_ge(last_ready, 1)
            pool.wait_ge(chain, steps_all)
            pool.wait_ge(mended_out, 16)
            pool.wait_ge(zero_out, 16)
            for g, (a, z) in enumerate(spans):
                for j in range(a, z):
                    nc.gpsimd.indirect_dma_start(
                        rows[:, j, :], None, running[:, :],
                        bass.IndirectOffsetOnAxis(last_edge[:, j:j + 1], 0)).then_inc(final_in[g], 16)

        @block.tensor
        def _(pe):
            pe.wait_ge(ident_set, 1)
            pe.wait_ge(w_ready, 1)
            nc.tensor.transpose(t_ps[0][:, 0:D], w_sb[:, D:2 * D], ident[:, :])
            nc.tensor.transpose(t_ps[0][:, D:2 * D], w_diff[:, :], ident[:, :]).then_inc(wT_made, 1)

            def transposes(g):
                a, z = spans[g]
                if len(shares(g)[0]):
                    pe.wait_ge(xn_pool, sum(len(shares(i)[0]) > 0 for i in range(g + 1)))
                pe.wait_ge(xn_dve, g + 1)
                pe.wait_ge(xn_act, g + 1)
                if g == 0:
                    pe.wait_ge(wT_ready, 1)
                if g >= 2:
                    pe.wait_ge(hT_ready, g - 1)
                for i in range(z - a):
                    last = nc.tensor.transpose(t_ps[g % 2][:, i * D:(i + 1) * D], xn[:, g % 2, i, :], ident[:, :])
                last.then_inc(xT_made, 1)

            def products(g, which, made, turn):
                a, z = spans[g]
                for j in range(a, z):
                    last = nc.tensor.matmul(m_ps[turn % 2][:, (j - a) * D:(j - a + 1) * D], hT[:, j * P:(j + 1) * P],
                                            wT[:, which, :], start=True, stop=True)
                last.then_inc(made, 1)

            def near_products(g):
                pe.wait_ge(hT_ready, g + 1)
                if g >= 2:
                    pe.wait_ge(near_ready, g - 1)
                products(g, 0, near_made, g)

            transposes(0)
            for g in range(1, groups):
                transposes(g)
                near_products(g - 1)
            near_products(groups - 1)
            for g in range(groups):
                turn = groups + g
                if g < 2:
                    pe.wait_ge(near_ready, turn - 1)
                else:
                    pe.wait_ge(self_ready, g - 1)
                products(g, 1, self_made, turn)

            pe.wait_ge(self_ready, groups)
            nc.tensor.matmul(count_ps, zeros_b[:, :], zeros_b[:, 0:tiles], start=True, stop=False,
                             skip_group_check=True).then_inc(count_open, 1)

            def blocks(k, sizes):
                for s, n in enumerate(sizes):
                    pe.wait_ge(flags_ready, k * SLOTS + (s + 1))
                    for t in range(n):
                        last = nc.tensor.matmul(count_ps, le[:, s % 2, t, :], eq[:, s % 2, t, :], start=False,
                                                stop=False, skip_group_check=True)
                    last.then_inc(counted, 1)

            pe.wait_ge(count_open, 1)
            with pe.Fori(0, turns) as k:
                blocks(k, FULL_TURN)
            blocks(turns, LAST_TURN)
            pe.wait_ge(counted, blocks_all)
            nc.tensor.matmul(count_ps, zeros_b[:, :], zeros_b[:, 0:tiles], start=False, stop=True,
                             skip_group_check=True).then_inc(count_done, 1)
            pe.wait_ge(evacuated, blocks_all)
            nc.tensor.transpose(tailT_ps, maxima[:, last_half, LAST_TURN[-1] - 1, :], ident[:, :]).then_inc(tailT_made, 1)
            pe.wait_ge(whole_ready, 1)
            nc.tensor.matmul(whole_ps, ones[:, :], whole_diag[:, :], start=True, stop=True).then_inc(whole_made, 1)
            pe.wait_ge(counts_ready, 1)
            nc.tensor.matmul(totals_ps, last_row[:, :], counts[:, :], start=True, stop=True)
            nc.tensor.matmul(degree_ps, step_down[:, :], counts[:, :], start=True, stop=True).then_inc(totals_made, 1)
            pe.wait_ge(carried_ready, 1)
            nc.tensor.transpose(carry_ps, carried_T[:, 0:P], ident[:, :]).then_inc(carry_made, 1)

        @block.vector
        def _(dve):
            own = [0]

            def then(ins):
                own[0] += 1
                ins.then_inc(dve_step, 1)

            def settled():
                dve.wait_ge(dve_step, own[0])

            nc.vector.memset(eps[:, :], EPS).then_inc(eps_set, 1)
            nc.vector.memset(zero_f[:, :], 0.0).then_inc(zero_set, 1)
            then(nc.vector.memset(ones[:, :], 1.0))
            dve.wait_ge(iota_set, 2)
            then(nc.vector.tensor_copy(iota_f[:, :], iota_i[:, :]))
            then(nc.vector.tensor_copy(part_f[:, :], part_i[:, :]))
            settled()
            then(nc.vector.tensor_scalar(ident[:, :], iota_f[:, :], part_f[:, 0:1], None, ALU.is_equal))
            settled()
            nc.vector.memset(zeros_b[:, :], 0.0).then_inc(ident_set, 1)
            dve.wait_ge(w_in, 16)
            nc.vector.tensor_tensor(w_diff[:, :], w_sb[:, 0:D], w_sb[:, D:2 * D], ALU.subtract).then_inc(w_ready, 1)

            def statistics(g):
                a, z = spans[g]
                dve.wait_ge(x_in[g], 32 if g == groups - 1 else 16)
                for j in range(a, z):
                    then(nc.vector.bn_stats(stats[:, g % 2, j - a, :], xs[:, j, :]))
                settled()
                for j in range(a, z):
                    last = nc.vector.bn_aggr(mv[:, j, :], stats[:, g % 2, j - a, :])
                last.then_inc(var_ready, 1)

            def normalise(g):
                at = slice(*spans[g])
                dve.wait_ge(std_ready, g + 1)
                then(nc.vector.reciprocal(rstd[:, at], std[:, at]))
                settled()
                nc.vector.scalar_tensor_tensor(shift[:, at], mv[:, at, 0], -1.0, rstd[:, at],
                                               ALU.mult, ALU.mult).then_inc(rstd_ready, 1)
                if g >= 2:
                    dve.wait_ge(xT_made, g - 1)
                for j in shares(g)[1]:
                    last = nc.vector.tensor_scalar(xn[:, g % 2, j - spans[g][0], :], xs[:, j, :], mv[:, j, 0:1],
                                                   rstd[:, j:j + 1], ALU.subtract, ALU.mult)
                last.then_inc(xn_dve, 1)

            statistics(0)
            for g in range(groups):
                if g + 1 < groups:
                    statistics(g + 1)
                normalise(g)

            dve.wait_ge(bias_in, 16)
            dve.wait_ge(near_out, 16 * groups)
            for g, (a, z) in enumerate(spans):
                dve.wait_ge(self_made, g + 1)
                nc.vector.tensor_tensor(dense[:, a:z, :],
                                        m_ps[(groups + g) % 2][:, 0:(z - a) * D].rearrange("p (j d) -> p j d", d=D),
                                        bias[:, None, :].to_broadcast([P, z - a, D]), ALU.add).then_inc(self_ready, 1)

            dve.wait_ge(dst_in, 48)
            then(nc.vector.tensor_copy(dst_f[:, :], dst_sb[:, :]))
            settled()
            then(nc.vector.tensor_tensor(fresh[:, 1:cols], dst_f[:, 1:cols], dst_f[:, 0:cols - 1], ALU.not_equal))
            then(nc.vector.memset(fresh[:, 0:1], 1.0))
            settled()
            then(nc.vector.tensor_scalar(fresh[:, :], fresh[:, :], LOW, None, ALU.mult))
            then(nc.vector.tensor_scalar(lo_i[:, :], dst_sb[:, :], P - 1, None, ALU.bitwise_and))
            settled()
            then(nc.vector.tensor_copy(lo[:, :], lo_i[:, :]))
            settled()
            then(nc.vector.tensor_scalar(lo_i[:, :], dst_sb[:, :], P.bit_length() - 1, None, ALU.logical_shift_right))
            settled()
            then(nc.vector.tensor_copy(hi[:, :], lo_i[:, :]))
            dve.wait_ge(self_ready, groups)
            then(nc.vector.tensor_copy(iota_ps, iota_f[:, :]))
            then(nc.vector.memset(run_ps(1, STEPS - 1), LOW))
            settled()

            def blocks(k, first, sizes):
                for s, n in enumerate(sizes):
                    blk = k * SLOTS + s
                    h = s % 2
                    base = blk * CH
                    if not (first and s < 2):
                        dve.wait_ge(counted, blk - 1)
                    at = bass.ds(blk * STEPS, n)
                    nc.vector.tensor_tensor(le[:, h, 0:n, :], iota_ps[:, None, :].to_broadcast([P, n, P]),
                                            lo[:, at, None].to_broadcast([P, n, P]), ALU.is_ge)
                    nc.vector.tensor_tensor(eq[:, h, 0:n, :], iota_ps[:, None, 0:tiles].to_broadcast([P, n, tiles]),
                                            hi[:, at, None].to_broadcast([P, n, tiles]),
                                            ALU.is_equal).then_inc(flags_ready, 1)
                    if not (first and s == 0):
                        dve.wait_ge(chain, base)
                    nc.vector.tensor_scalar(fresh_blk[:, h, 0:n], fresh[:, bass.ds(blk * STEPS, n)], 0.0, None,
                                            ALU.add).then_inc(chain, 1)
                    if not (first and s == 0):
                        dve.wait_ge(evacuated, blk)
                    dve.wait_ge(gathered[s], k * (16 * STEPS) + 16 * n)
                    for t in range(n):
                        before_ps = run_ps(h, t - 1) if t else run_ps(1 - h, STEPS - 1)
                        dve.wait_ge(chain, base + (t + 1))
                        nc.vector.scalar_tensor_tensor(run_ps(h, t), before_ps, fresh_blk[:, h, t:t + 1],
                                                       rows[:, s * STEPS + t, :], ALU.add, ALU.max).then_inc(chain, 1)
            then(nc.vector.tensor_copy(before[:, :], before_i[:, 0:1]))
            then(nc.vector.tensor_scalar(lo_i[:, :], dst_f[:, :], dst_f[:, 0:1], None, ALU.is_equal))
            settled()
            then(nc.vector.reduce_sum(run[:, :], lo_i[:, :], AX.X))
            then(nc.vector.tensor_tensor(linked[:, :], before[:, :], dst_f[:, 0:1], ALU.is_equal))
            settled()
            then(nc.vector.tensor_scalar(linked_low[:, :], linked[:, :], 1.0, -LOW, ALU.subtract, ALU.mult))
            then(nc.vector.scalar_tensor_tensor(whole[:, :], run[:, :], float(cols), linked[:, :], ALU.is_equal, ALU.mult))
            then(nc.vector.tensor_scalar(mend_f[:, :], part_f[:, :], float(cols), -1.0, ALU.mult, ALU.add))
            settled()
            nc.vector.tensor_scalar(whole_diag[:, :], ident[:, :], whole[:, 0:1], None, ALU.mult).then_inc(whole_ready, 1)
            nc.vector.tensor_tensor(mend_idx[:, :], mend_f[:, :], run[:, :], ALU.add).then_inc(mend_idx_ready, 1)
            then(nc.vector.tensor_scalar(step_down[:, :], iota_f[:, :], part_f[:, 0:1], 1.0, ALU.subtract, ALU.is_equal))
            then(nc.vector.tensor_scalar(whole_low[:, 0:1], part_f[:, :], float(P - 1), None, ALU.is_equal))
            settled()
            then(nc.vector.tensor_tensor(step_down[:, :], ident[:, :], step_down[:, :], ALU.subtract))
            then(nc.vector.tensor_scalar(last_row[:, :], ones[:, :], whole_low[:, 0:1], None, ALU.mult))
            settled()

            blocks(0, True, FULL_TURN)
            with dve.Fori(1, turns) as k:
                blocks(k, False, FULL_TURN)
            blocks(turns, False, LAST_TURN)

            dve.wait_ge(whole_made, 1)
            then(nc.vector.tensor_scalar(whole_low[:, :], whole_ps, 1.0, -LOW, ALU.subtract, ALU.mult))
            dve.wait_ge(tailT_made, 1)
            then(nc.vector.tensor_copy(tails_T[:, :], tailT_ps))
            then(nc.vector.memset(carried_T[:, 0:1], 0.0))
            settled()
            nc.vector.tensor_tensor_scan(carried_T[:, 1:P + 1], whole_low[:, :], tails_T[:, :], LOW,
                                         ALU.add, ALU.max).then_inc(carried_ready, 1)
            dve.wait_ge(count_done, 1)
            nc.vector.tensor_copy(counts[:, :], count_ps).then_inc(counts_ready, 1)
            dve.wait_ge(mend_in, 16)
            dve.wait_ge(carry_made, 1)
            nc.vector.scalar_tensor_tensor(mended[:, :], carry_ps, linked_low[:, 0:1], mend[:, :],
                                           ALU.add, ALU.max).then_inc(mended_ready, 1)
            dve.wait_ge(totals_made, 1)
            then(nc.vector.tensor_copy(ends[:, :], totals_ps))
            then(nc.vector.tensor_scalar(has_edges[:, :], degree_ps, 0.0, None, ALU.is_gt))
            settled()
            then(nc.vector.tensor_tensor_scan(upto[:, :], ones[:, 0:tiles], ends[:, :], 0.0, ALU.mult, ALU.add))
            settled()
            then(nc.vector.tensor_tensor(upto[:, :], upto[:, :], ends[:, :], ALU.subtract))
            settled()
            then(nc.vector.tensor_tensor(upto[:, :], upto[:, :], counts[:, :], ALU.add))
            settled()
            then(nc.vector.tensor_scalar(last_f[:, :], upto[:, :], float(-1 - zero_row), None, ALU.add))
            settled()
            then(nc.vector.tensor_tensor(last_f[:, :], last_f[:, :], has_edges[:, :], ALU.mult))
            settled()
            nc.vector.tensor_scalar(last_edge[:, :], last_f[:, :], float(zero_row), None, ALU.add).then_inc(last_ready, 1)

            then(nc.vector.tensor_tensor(dense[:, :, :], dense[:, :, :],
                                         has_edges[:, :, None].to_broadcast([P, tiles, D]), ALU.mult))
            settled()
            then(nc.vector.tensor_tensor(dense[:, :, :], dense[:, :, :], xs[:, :, :], ALU.add))
            settled()
            for g, (a, z) in enumerate(spans):
                dve.wait_ge(final_in[g], 16 * (z - a))
                nc.vector.tensor_tensor(rows[:, a:z, :], rows[:, a:z, :], dense[:, a:z, :],
                                        ALU.add).then_inc(final_ready, 1)


def kernel(**inputs):
    import numpy as np
    import concourse.bacc as bacc
    from concourse.bass_utils import run_bass_kernel_spmd as run

    nc = bacc.Bacc("TRN2", target_bir_lowering=False, num_devices=1)
    arrays, args = {}, []
    for name in ["x", "src", "dst", "L0_gnn_W", "L0_gnn_b"]:
        a = np.ascontiguousarray(inputs[name])
        arrays[f"in_{name}"] = a
        args.append(nc.dram_tensor(f"in_{name}", a.shape, mybir.dt.from_np(a.dtype), kind="ExternalInput").ap())
    args.append(nc.dram_tensor("out_x", inputs["x"].shape, F32, kind="ExternalOutput").ap())
    edgeconv(nc, *args)
    return run(nc, [arrays], core_ids=[0]).results[0]["out_x"]
```

```python
from contextlib import ExitStack

import concourse.bass as bass
from concourse import mybir

P = 128
F32 = mybir.dt.float32
BF16 = mybir.dt.bfloat16
I32 = mybir.dt.int32
ALU = mybir.AluOpType
ACT = mybir.ActivationFunctionType
AX = mybir.AxisListType

EPS = 1e-5
LOW = -3.0e38
GROUP = 8
STEPS = 12
SLOTS = 4


def edgeconv(nc, x, src, dst, W, b, out):
    nodes, D = x.shape
    edges = src.shape[0]
    tiles = -(-nodes // P)
    sizes = [4] + [GROUP] * ((tiles - 4 - 5) // GROUP)
    sizes += [tiles - sum(sizes) - 2, 2] if tiles - sum(sizes) > 2 else [tiles - sum(sizes)]
    spans = [(sum(sizes[:g]), sum(sizes[:g + 1])) for g in range(len(sizes))]
    groups = len(spans)
    full = nodes // P
    rest = nodes - full * P
    cols = -(-edges // P)
    turns = (cols - SLOTS) // (STEPS * SLOTS)
    FULL_TURN = [STEPS] * SLOTS
    LAST_TURN = []
    left = cols - turns * STEPS * SLOTS
    for s in range(SLOTS):
        LAST_TURN.append(min(STEPS, left - (SLOTS - 1 - s), -(-left * 2 // 5) if s < SLOTS - 1 else left))
        left -= LAST_TURN[-1]
    blocks_all = (turns + 1) * SLOTS
    steps_all = cols + blocks_all
    last_half = (SLOTS - 1) % 2
    tail = edges - (P - 1) * cols
    assert D == P and max(sizes) <= GROUP and 0 < tail <= cols and rest and tiles == full + 1
    assert turns > 2 and left == 0 and min(LAST_TURN) > 0 and SLOTS % 2 == 0

    near = nc.dram_tensor("near_table", (tiles * P, D), F32, kind="Internal").ap()
    running = nc.dram_tensor("running_max", (P * cols + 1, D), F32, kind="Internal").ap()
    zero_row = P * cols
    running_by_part = running[0:P * cols, :].rearrange("(p t) d -> p t d", p=P)
    x_tiles = x[0:full * P, :].rearrange("(j p) d -> p j d", p=P)
    out_tiles = out[0:full * P, :].rearrange("(j p) d -> p j d", p=P)
    near_tiles = near.rearrange("(j p) d -> p j d", p=P)

    with ExitStack() as ctx:
        def sb(name, shape, dt):
            return ctx.enter_context(nc.sbuf_tensor(name, shape, dt))

        def sem(name):
            return ctx.enter_context(nc.semaphore(name))

        xs = sb("xs", [P, tiles, D], F32)
        hT = sb("hT", [P, tiles * P], F32)
        dense = sb("dense", [P, tiles, D], F32)
        xn = sb("xn", [P, 2, GROUP, D], F32)
        stats = sb("stats", [P, 2, GROUP, 6], F32)
        mv = sb("mv", [P, tiles, 2], F32)
        std = sb("std", [P, tiles], F32)
        eps = sb("eps", [P, 1], F32)
        rstd = sb("rstd", [P, tiles], F32)
        shift = sb("shift", [P, tiles], F32)
        w_sb = sb("w_sb", [P, 2 * D], F32)
        w_diff = sb("w_diff", [P, D], F32)
        wT = sb("wT", [P, 2, D], F32)
        bias = sb("bias", [P, D], F32)
        iota_i = sb("iota_i", [P, P], I32)
        part_i = sb("part_i", [P, 1], I32)
        iota_f = sb("iota_f", [P, P], F32)
        part_f = sb("part_f", [P, 1], F32)
        ident = sb("ident", [P, P], F32)
        step_down = sb("step_down", [P, P], F32)
        ones = sb("ones", [P, P], F32)
        last_row = sb("last_row", [P, P], F32)
        zero_f = sb("zero_f", [1, D], F32)
        zeros_b = sb("zeros_b", [P, P], BF16)

        src_sb = sb("src_sb", [P, cols], I32)
        dst_sb = sb("dst_sb", [P, cols], I32)
        dst_f = sb("dst_f", [P, cols], F32)
        fresh = sb("fresh", [P, cols], F32)
        lo_i = sb("lo_i", [P, cols], I32)
        lo = sb("lo", [P, cols], BF16)
        hi = sb("hi", [P, cols], BF16)
        before_i = sb("before_i", [P, 2], I32)
        before = sb("before", [P, 1], F32)
        run = sb("run", [P, 1], F32)
        linked = sb("linked", [P, 1], F32)
        linked_low = sb("linked_low", [P, 1], F32)
        whole = sb("whole", [P, 1], F32)
        whole_diag = sb("whole_diag", [P, P], F32)
        whole_low = sb("whole_low", [P, P], F32)
        mend_f = sb("mend_f", [P, 1], F32)
        mend_idx = sb("mend_idx", [P, 1], I32)

        drops = sb("drops", [P, 1], F32)
        drop = sb("drop", [P, 1], F32)
        disorder = sb("disorder", [P, 1], I32)
        idx = sb("idx", [P, SLOTS, STEPS], I32)
        rows = sb("rows", [P, max(tiles, SLOTS * STEPS), D], F32)
        fresh_blk = sb("fresh_blk", [P, 2, STEPS], F32)
        maxima = sb("maxima", [P, 2, STEPS, D], F32)
        le = sb("le", [P, 2, STEPS, P], BF16)
        eq = sb("eq", [P, 2, STEPS, tiles], BF16)

        counts = sb("counts", [P, tiles], F32)
        ends = sb("ends", [P, tiles], F32)
        upto = sb("upto", [P, tiles], F32)
        has_edges = sb("has_edges", [P, tiles], F32)
        last_f = sb("last_f", [P, tiles], F32)
        last_edge = sb("last_edge", [P, tiles], I32)
        tails_T = sb("tails_T", [P, P], F32)
        carried_T = sb("carried_T", [P, P + 1], F32)
        mend = sb("mend", [P, D], F32)
        mended = sb("mended", [P, D], F32)

        ps = ctx.enter_context(nc.psum_tensor("ps", [P, 8 * 512], F32))
        t_ps = [ps[:, i * 1024:(i + 1) * 1024] for i in range(2)]
        m_ps = [ps[:, 2048 + i * 1024:2048 + (i + 1) * 1024] for i in range(2)]

        def run_ps(h, t):
            at = (h * STEPS + t) * D
            return ps[:, at:at + D]

        iota_ps = ps[:, 6 * 512:6 * 512 + P]
        count_ps = ps[:, 7 * 512:7 * 512 + tiles]
        totals_ps = ps[:, 0:tiles]
        degree_ps = ps[:, 512:512 + tiles]
        tailT_ps = ps[:, 1024:1024 + P]
        carry_ps = ps[:, 1536:1536 + P]
        drops_ps = ps[:, 6 * 512 + P:6 * 512 + P + 1]
        whole_ps = ps[:, 7 * 512 + 128:7 * 512 + 256]

        x_pad_set = sem("x_pad_set")
        edge_pad_set = sem("edge_pad_set")
        x_in = [sem(f"x_in{g}") for g in range(groups)]
        w_in = sem("w_in")
        bias_in = sem("bias_in")
        src_in = sem("src_in")
        dst_in = sem("dst_in")
        iota_set = sem("iota_set")
        dve_step = sem("dve_step")
        ident_set = sem("ident_set")
        w_ready = sem("w_ready")
        wT_made = sem("wT_made")
        wT_ready = sem("wT_ready")
        eps_set = sem("eps_set")
        var_ready = sem("var_ready")
        std_ready = sem("std_ready")
        rstd_ready = sem("rstd_ready")
        xn_pool = sem("xn_pool")
        xn_act = sem("xn_act")
        xn_dve = sem("xn_dve")
        xT_made = sem("xT_made")
        hT_ready = sem("hT_ready")
        near_made = sem("near_made")
        near_ready = sem("near_ready")
        near_out = sem("near_out")
        self_made = sem("self_made")
        self_ready = sem("self_ready")
        idx_in = [sem(f"idx_in{s}") for s in range(SLOTS)]
        block_begun = sem("block_begun")
        gathered = [sem(f"gathered{s}") for s in range(SLOTS)]
        chain = sem("chain")
        evacuated = sem("evacuated")
        maxima_out = [sem(f"maxima_out{h}") for h in range(2)]
        flags_ready = sem("flags_ready")
        counted = sem("counted")
        count_open = sem("count_open")
        count_done = sem("count_done")
        counts_ready = sem("counts_ready")
        totals_made = sem("totals_made")
        last_ready = sem("last_ready")
        mend_idx_ready = sem("mend_idx_ready")
        whole_ready = sem("whole_ready")
        whole_made = sem("whole_made")
        tailT_made = sem("tailT_made")
        carried_ready = sem("carried_ready")
        carry_made = sem("carry_made")
        mend_in = sem("mend_in")
        mended_ready = sem("mended_ready")
        mended_out = sem("mended_out")
        drops_ready = sem("drops_ready")
        drops_made = sem("drops_made")
        disorder_ready = sem("disorder_ready")
        turned_in = sem("turned_in")
        edges_in = sem("edges_in")
        turned_out = sem("turned_out")
        zero_set = sem("zero_set")
        zero_out = sem("zero_out")
        final_in = [sem(f"final_in{g}") for g in range(groups)]
        final_ready = sem("final_ready")
        out_done = sem("out_done")

        block = ctx.enter_context(nc.Block())

        def edge_at(k, sizes, s):
            return k * (STEPS * SLOTS) + sum(sizes[:s])

        def chain_at(k, sizes, s):
            return k * ((STEPS + 1) * SLOTS) + (sum(sizes[:s]) + s)

        def shares(g):
            a, z = spans[g]
            p = a + 3 * (z - a) // 8
            v = p + max(1, 3 * (z - a) // 8)
            return range(a, p), range(p, v), range(v, z)



        @block.sync
        def _(sp):
            sp.dma_start(xs[:, 0:spans[0][1], :], x_tiles[:, 0:spans[0][1], :]).then_inc(x_in[0], 16)
            for g in range(1, groups):
                a, z = spans[g]
                z = min(full, z)
                sp.dma_start(xs[:, a:z, :], x_tiles[:, a:z, :]).then_inc(x_in[g], 16)
            sp.wait_ge(x_pad_set, 1)
            sp.dma_start(xs[0:rest, full, :], x[full * P:nodes, :]).then_inc(x_in[groups - 1], 16)
            sp.wait_ge(edge_pad_set, 3)
            by_part = (P - 1) * cols
            sp.dma_start(src_sb[0:P - 1, :], src[0:by_part].rearrange("(p t) -> p t", t=cols)).then_inc(src_in, 16)
            sp.dma_start(src_sb[P - 1:P, 0:tail], src[by_part:edges][None, :]).then_inc(src_in, 16)
            sp.dma_start(dst_sb[0:P - 1, :], dst[0:by_part].rearrange("(p t) -> p t", t=cols)).then_inc(dst_in, 16)
            sp.dma_start(dst_sb[P - 1:P, 0:tail], dst[by_part:edges][None, :]).then_inc(dst_in, 16)
            sp.dma_start(before_i[1:P, :], bass.AP(dst.tensor, dst.offset + cols - 1,
                                                   [[cols, P - 1], [1, 2]])).then_inc(dst_in, 16)

            def indices(k, sizes, s):
                n = sizes[s]
                sp.dma_start(idx[:, s, 0:n], src_sb[:, bass.ds(edge_at(k, sizes, s), n)]).then_inc(idx_in[s], 16)

            def blocks(k, sizes, following):
                for s, n in enumerate(sizes):
                    if following:
                        sp.wait_ge(chain, chain_at(k, sizes, s) + (n + 1))
                        indices(k + 1, following, s)
                    sp.wait_ge(evacuated, k * SLOTS + (s + 1))
                    sp.dma_start(running_by_part[:, bass.ds(edge_at(k, sizes, s), n), :],
                                 maxima[:, s % 2, 0:n, :]).then_inc(maxima_out[s % 2], 16)

            for g, (a, z) in enumerate(spans):
                if g == groups // 2:
                    sp.wait_ge(src_in, 32)
                    for s in range(SLOTS):
                        indices(0, FULL_TURN, s)
                sp.wait_ge(near_ready, g + 1)
                sp.dma_start(near_tiles[:, a:z, :], dense[:, a:z, :]).then_inc(near_out, 16)
            sp.wait_ge(zero_set, 1)
            sp.dma_start(running[zero_row:zero_row + 1, :], zero_f[:, :]).then_inc(zero_out, 16)
            with sp.Fori(0, turns - 1) as k:
                blocks(k, FULL_TURN, FULL_TURN)
            blocks(turns - 1, FULL_TURN, LAST_TURN)
            blocks(turns, LAST_TURN, [])

            for g, (a, z) in enumerate(spans):
                sp.wait_ge(final_ready, g + 1)
                z = min(full, z)
                sp.dma_start(out_tiles[:, a:z, :], rows[:, a:z, :]).then_inc(out_done, 16)
            sp.dma_start(out[full * P:nodes, :], rows[0:rest, full, :]).then_inc(out_done, 16)
            sp.wait_ge(out_done, 16 * (groups + 1))

        @block.scalar
        def _(act):
            act.dma_start(w_sb[:, :], W).then_inc(w_in, 16)
            act.dma_start(bias[:, :], b[None, :].to_broadcast([P, D])).then_inc(bias_in, 16)

            act.wait_ge(wT_made, 1)
            nc.scalar.copy(wT[:, :, :].rearrange("p a d -> p (a d)"), t_ps[0][:, 0:2 * D]).then_inc(wT_ready, 1)

            def deviations(g):
                at = slice(*spans[g])
                act.wait_ge(var_ready, g + 1)
                nc.scalar.activation(std[:, at], mv[:, at, 1], ACT.Sqrt, bias=eps[:, 0:1]).then_inc(std_ready, 1)

            def normalise(g):
                act.wait_ge(rstd_ready, g + 1)
                if g >= 2:
                    act.wait_ge(xT_made, g - 1)
                for j in shares(g)[2]:
                    last = nc.scalar.activation(xn[:, g % 2, j - spans[g][0], :], xs[:, j, :], ACT.Identity,
                                                bias=shift[:, j:j + 1], scale=rstd[:, j:j + 1])
                last.then_inc(xn_act, 1)

            def relu(g):
                a, z = spans[g]
                act.wait_ge(xT_made, g + 1)
                nc.scalar.activation(hT[:, a * P:z * P], t_ps[g % 2][:, 0:(z - a) * P], ACT.Relu).then_inc(hT_ready, 1)

            def near_copy(g):
                a, z = spans[g]
                act.wait_ge(near_made, g + 1)
                nc.scalar.copy(dense[:, a:z, :].rearrange("p j d -> p (j d)"),
                               m_ps[g % 2][:, 0:(z - a) * D]).then_inc(near_ready, 1)

            act.wait_ge(eps_set, 1)
            deviations(0)
            for g in range(groups + 2):
                if 1 <= g <= groups:
                    relu(g - 1)
                if g + 1 < groups:
                    deviations(g + 1)
                if g < groups:
                    normalise(g)
                if g >= 2:
                    near_copy(g - 2)

            def blocks(k, first, sizes):
                for s, n in enumerate(sizes):
                    h = s % 2
                    if not (first and s < 2):
                        act.wait_ge(maxima_out[h], (k * (SLOTS // 2) + s // 2) * 16)
                    act.wait_ge(chain, chain_at(k, sizes, s) + (n + 1))
                    half = ps[:, h * STEPS * D:(h * STEPS + n) * D]
                    nc.scalar.copy(maxima[:, h, 0:n, :].rearrange("p t d -> p (t d)"), half).then_inc(evacuated, 1)

            blocks(0, True, FULL_TURN)
            with act.Fori(1, turns) as k:
                blocks(k, False, FULL_TURN)
            blocks(turns, False, LAST_TURN)

        def edge_by_edge(pool):
            HALF = P // 2
            CHUNK = GROUP * D
            near_T = hT
            best_T = rows[:, 0:tiles, :].rearrange("p j d -> p (j d)")
            edge_src = xn[0:1, 0, :, :].rearrange("p i d -> p (i d)").bitcast(I32)
            edge_dst = xn[0:1, 1, :, :].rearrange("p i d -> p (i d)").bitcast(I32)

            of_src, of_dst, larger = (mended[:, i:i + 1] for i in range(3))

            nc.gpsimd.memset(best_T, LOW)
            with pool.Fori(0, 2 * tiles) as i:
                with nc.allow_non_contiguous_dma(reason="a transpose that only unsorted edges need"):
                    nc.gpsimd.dma_start(near_T[:, bass.ds(i * HALF, HALF)],
                                        near[bass.ds(i * HALF, HALF), :].rearrange("n d -> d n")).then_inc(turned_in, 16)
                pool.wait_ge(turned_in, i * 16 + 16)
                pool.sem_inc(block_begun, 1)

            def chunk(at, n, so_far):
                nc.gpsimd.dma_start(edge_src[:, 0:n], src[bass.ds(at, n)][None, :]).then_inc(edges_in, 16)
                nc.gpsimd.dma_start(edge_dst[:, 0:n], dst[bass.ds(at, n)][None, :]).then_inc(edges_in, 16)
                pool.wait_ge(edges_in, so_far)
                pool.sem_inc(block_begun, 1)
                with pool.Fori(0, n) as e:
                    s = pool.value_load(edge_src[:, bass.ds(e, 1)], min_val=0, max_val=nodes - 1)
                    d = pool.value_load(edge_dst[:, bass.ds(e, 1)], min_val=0, max_val=nodes - 1)
                    pool.drain()
                    nc.gpsimd.tensor_copy(of_src, near_T[:, bass.ds(s, 1)])
                    nc.gpsimd.tensor_copy(of_dst, best_T[:, bass.ds(d, 1)])
                    pool.drain()
                    nc.gpsimd.tensor_scalar(larger, of_dst, of_src, None, ALU.max)
                    pool.drain()
                    nc.gpsimd.tensor_copy(best_T[:, bass.ds(d, 1)], larger)

            with pool.Fori(0, edges // CHUNK) as c:
                chunk(c * CHUNK, CHUNK, c * 32 + 32)
            if edges % CHUNK:
                chunk(edges // CHUNK * CHUNK, edges % CHUNK, (edges // CHUNK + 1) * 32)
            pool.drain()
            nc.gpsimd.tensor_scalar(near_T[:, :], best_T, LOW / 2, None, ALU.is_gt)
            pool.drain()
            nc.gpsimd.tensor_tensor(best_T, best_T, near_T[:, :], ALU.mult)
            pool.drain()
            with pool.Fori(0, 2 * tiles) as i:
                with nc.allow_non_contiguous_dma(reason="a transpose that only unsorted edges need"):
                    nc.gpsimd.dma_start(running[bass.ds(i * HALF, HALF), :].rearrange("n d -> d n"),
                                        best_T[:, bass.ds(i * HALF, HALF)]).then_inc(turned_out, 16)
                pool.wait_ge(turned_out, i * 16 + 16)
                pool.sem_inc(block_begun, 1)
            nc.gpsimd.iota(last_edge[:, :], [[P, tiles]], base=0, channel_multiplier=1)
            pool.drain()

        @block.gpsimd
        def _(pool):
            nc.gpsimd.memset(xs[:, full, :], 0.0).then_inc(x_pad_set, 1)
            nc.gpsimd.memset(dst_sb[:, tail:cols], 64 * P - 1).then_inc(edge_pad_set, 1)
            nc.gpsimd.memset(src_sb[:, tail:cols], 0).then_inc(edge_pad_set, 1)
            nc.gpsimd.memset(before_i[:, :], -1).then_inc(edge_pad_set, 1)
            nc.gpsimd.iota(iota_i[:, :], [[1, P]], base=0, channel_multiplier=0).then_inc(iota_set, 1)
            nc.gpsimd.iota(part_i[:, :], [[0, 1]], base=0, channel_multiplier=1).then_inc(iota_set, 1)
            for g in range(groups):
                if len(shares(g)[0]):
                    pool.wait_ge(rstd_ready, g + 1)
                    if g >= 2:
                        pool.wait_ge(xT_made, g - 1)
                    for j in shares(g)[0]:
                        last = nc.gpsimd.tensor_scalar(xn[:, g % 2, j - spans[g][0], :], xs[:, j, :], mv[:, j, 0:1],
                                                       rstd[:, j:j + 1], ALU.subtract, ALU.mult)
                    last.then_inc(xn_pool, 1)

            pool.wait_ge(near_out, 16 * groups)

            def blocks(k, sizes):
                for s, n in enumerate(sizes):
                    pool.wait_ge(idx_in[s], k * 16 + 16)
                    pool.sem_inc(block_begun, 1)
                    for t in range(n):
                        nc.gpsimd.indirect_dma_start(
                            rows[:, s * STEPS + t, :], None, near[:, :],
                            bass.IndirectOffsetOnAxis(idx[:, s, t:t + 1], 0)).then_inc(gathered[s], 16)

            with pool.Fori(0, turns) as k:
                blocks(k, FULL_TURN)
            blocks(turns, LAST_TURN)

            pool.wait_ge(mend_idx_ready, 1)
            for h in range(2):
                pool.wait_ge(maxima_out[h], blocks_all // 2 * 16)
            nc.gpsimd.indirect_dma_start(mend[:, :], None, running[:, :],
                                         bass.IndirectOffsetOnAxis(mend_idx[:, 0:1], 0)).then_inc(mend_in, 16)
            pool.wait_ge(mended_ready, 1)
            nc.gpsimd.indirect_dma_start(running[:, :], bass.IndirectOffsetOnAxis(mend_idx[:, 0:1], 0),
                                         mended[:, :], None).then_inc(mended_out, 16)
            pool.wait_ge(last_ready, 1)
            pool.wait_ge(chain, steps_all)
            pool.wait_ge(mended_out, 16)
            pool.wait_ge(zero_out, 16)
            pool.wait_ge(disorder_ready, 1)
            with pool.If(pool.value_load(disorder[0:1, 0:1], min_val=0, max_val=edges) > 0):
                edge_by_edge(pool)
            for g, (a, z) in enumerate(spans):
                for j in range(a, z):
                    nc.gpsimd.indirect_dma_start(
                        rows[:, j, :], None, running[:, :],
                        bass.IndirectOffsetOnAxis(last_edge[:, j:j + 1], 0)).then_inc(final_in[g], 16)

        @block.tensor
        def _(pe):
            pe.wait_ge(ident_set, 1)
            pe.wait_ge(w_ready, 1)
            nc.tensor.transpose(t_ps[0][:, 0:D], w_sb[:, D:2 * D], ident[:, :])
            nc.tensor.transpose(t_ps[0][:, D:2 * D], w_diff[:, :], ident[:, :]).then_inc(wT_made, 1)

            def transposes(g):
                a, z = spans[g]
                if len(shares(g)[0]):
                    pe.wait_ge(xn_pool, sum(len(shares(i)[0]) > 0 for i in range(g + 1)))
                pe.wait_ge(xn_dve, g + 1)
                pe.wait_ge(xn_act, g + 1)
                if g == 0:
                    pe.wait_ge(wT_ready, 1)
                if g >= 2:
                    pe.wait_ge(hT_ready, g - 1)
                for i in range(z - a):
                    last = nc.tensor.transpose(t_ps[g % 2][:, i * D:(i + 1) * D], xn[:, g % 2, i, :], ident[:, :])
                last.then_inc(xT_made, 1)

            def products(g, which, made, turn):
                a, z = spans[g]
                for j in range(a, z):
                    last = nc.tensor.matmul(m_ps[turn % 2][:, (j - a) * D:(j - a + 1) * D], hT[:, j * P:(j + 1) * P],
                                            wT[:, which, :], start=True, stop=True)
                last.then_inc(made, 1)

            def near_products(g):
                pe.wait_ge(hT_ready, g + 1)
                if g >= 2:
                    pe.wait_ge(near_ready, g - 1)
                products(g, 0, near_made, g)

            transposes(0)
            for g in range(1, groups):
                transposes(g)
                near_products(g - 1)
            near_products(groups - 1)
            for g in range(groups):
                turn = groups + g
                if g < 2:
                    pe.wait_ge(near_ready, turn - 1)
                else:
                    pe.wait_ge(self_ready, g - 1)
                products(g, 1, self_made, turn)

            pe.wait_ge(self_ready, groups)
            nc.tensor.matmul(count_ps, zeros_b[:, :], zeros_b[:, 0:tiles], start=True, stop=False,
                             skip_group_check=True).then_inc(count_open, 1)

            def blocks(k, sizes):
                for s, n in enumerate(sizes):
                    pe.wait_ge(flags_ready, k * SLOTS + (s + 1))
                    for t in range(n):
                        last = nc.tensor.matmul(count_ps, le[:, s % 2, t, :], eq[:, s % 2, t, :], start=False,
                                                stop=False, skip_group_check=True)
                    last.then_inc(counted, 1)

            pe.wait_ge(count_open, 1)
            with pe.Fori(0, turns) as k:
                blocks(k, FULL_TURN)
            blocks(turns, LAST_TURN)
            pe.wait_ge(counted, blocks_all)
            nc.tensor.matmul(count_ps, zeros_b[:, :], zeros_b[:, 0:tiles], start=False, stop=True,
                             skip_group_check=True).then_inc(count_done, 1)
            pe.wait_ge(evacuated, blocks_all)
            nc.tensor.transpose(tailT_ps, maxima[:, last_half, LAST_TURN[-1] - 1, :], ident[:, :]).then_inc(tailT_made, 1)
            pe.wait_ge(whole_ready, 1)
            nc.tensor.matmul(whole_ps, ones[:, :], whole_diag[:, :], start=True, stop=True).then_inc(whole_made, 1)
            pe.wait_ge(drops_ready, 1)
            nc.tensor.matmul(drops_ps, ones[:, :], drops[:, :], start=True, stop=True).then_inc(drops_made, 1)
            pe.wait_ge(counts_ready, 1)
            nc.tensor.matmul(totals_ps, last_row[:, :], counts[:, :], start=True, stop=True)
            nc.tensor.matmul(degree_ps, step_down[:, :], counts[:, :], start=True, stop=True).then_inc(totals_made, 1)
            pe.wait_ge(carried_ready, 1)
            nc.tensor.transpose(carry_ps, carried_T[:, 0:P], ident[:, :]).then_inc(carry_made, 1)

        @block.vector
        def _(dve):
            own = [0]

            def then(ins):
                own[0] += 1
                ins.then_inc(dve_step, 1)

            def settled():
                dve.wait_ge(dve_step, own[0])

            nc.vector.memset(eps[:, :], EPS).then_inc(eps_set, 1)
            nc.vector.memset(zero_f[:, :], 0.0).then_inc(zero_set, 1)
            then(nc.vector.memset(ones[:, :], 1.0))
            dve.wait_ge(iota_set, 2)
            then(nc.vector.tensor_copy(iota_f[:, :], iota_i[:, :]))
            then(nc.vector.tensor_copy(part_f[:, :], part_i[:, :]))
            settled()
            then(nc.vector.tensor_scalar(ident[:, :], iota_f[:, :], part_f[:, 0:1], None, ALU.is_equal))
            settled()
            nc.vector.memset(zeros_b[:, :], 0.0).then_inc(ident_set, 1)
            dve.wait_ge(w_in, 16)
            nc.vector.tensor_tensor(w_diff[:, :], w_sb[:, 0:D], w_sb[:, D:2 * D], ALU.subtract).then_inc(w_ready, 1)

            def statistics(g):
                a, z = spans[g]
                dve.wait_ge(x_in[g], 32 if g == groups - 1 else 16)
                for j in range(a, z):
                    then(nc.vector.bn_stats(stats[:, g % 2, j - a, :], xs[:, j, :]))
                settled()
                for j in range(a, z):
                    last = nc.vector.bn_aggr(mv[:, j, :], stats[:, g % 2, j - a, :])
                last.then_inc(var_ready, 1)

            def normalise(g):
                at = slice(*spans[g])
                dve.wait_ge(std_ready, g + 1)
                then(nc.vector.reciprocal(rstd[:, at], std[:, at]))
                settled()
                nc.vector.scalar_tensor_tensor(shift[:, at], mv[:, at, 0], -1.0, rstd[:, at],
                                               ALU.mult, ALU.mult).then_inc(rstd_ready, 1)
                if g >= 2:
                    dve.wait_ge(xT_made, g - 1)
                for j in shares(g)[1]:
                    last = nc.vector.tensor_scalar(xn[:, g % 2, j - spans[g][0], :], xs[:, j, :], mv[:, j, 0:1],
                                                   rstd[:, j:j + 1], ALU.subtract, ALU.mult)
                last.then_inc(xn_dve, 1)

            statistics(0)
            for g in range(groups):
                if g + 1 < groups:
                    statistics(g + 1)
                normalise(g)

            dve.wait_ge(bias_in, 16)
            dve.wait_ge(near_out, 16 * groups)
            for g, (a, z) in enumerate(spans):
                dve.wait_ge(self_made, g + 1)
                nc.vector.tensor_tensor(dense[:, a:z, :],
                                        m_ps[(groups + g) % 2][:, 0:(z - a) * D].rearrange("p (j d) -> p j d", d=D),
                                        bias[:, None, :].to_broadcast([P, z - a, D]), ALU.add).then_inc(self_ready, 1)

            dve.wait_ge(dst_in, 48)
            then(nc.vector.tensor_copy(dst_f[:, :], dst_sb[:, :]))
            settled()
            then(nc.vector.tensor_tensor(fresh[:, 1:cols], dst_f[:, 1:cols], dst_f[:, 0:cols - 1], ALU.not_equal))
            then(nc.vector.memset(fresh[:, 0:1], 1.0))
            settled()
            then(nc.vector.tensor_scalar(fresh[:, :], fresh[:, :], LOW, None, ALU.mult))
            then(nc.vector.tensor_scalar(lo_i[:, :], dst_sb[:, :], P - 1, None, ALU.bitwise_and))
            settled()
            then(nc.vector.tensor_copy(lo[:, :], lo_i[:, :]))
            settled()
            then(nc.vector.tensor_scalar(lo_i[:, :], dst_sb[:, :], P.bit_length() - 1, None, ALU.logical_shift_right))
            settled()
            then(nc.vector.tensor_copy(hi[:, :], lo_i[:, :]))
            dve.wait_ge(self_ready, groups)
            then(nc.vector.tensor_copy(iota_ps, iota_f[:, :]))
            then(nc.vector.memset(run_ps(1, STEPS - 1), LOW))
            settled()

            def blocks(k, first, sizes):
                for s, n in enumerate(sizes):
                    blk = k * SLOTS + s
                    h = s % 2
                    base = chain_at(k, sizes, s)
                    at = bass.ds(edge_at(k, sizes, s), n)
                    if not (first and s < 2):
                        dve.wait_ge(counted, blk - 1)
                    nc.vector.tensor_tensor(le[:, h, 0:n, :], iota_ps[:, None, :].to_broadcast([P, n, P]),
                                            lo[:, at, None].to_broadcast([P, n, P]), ALU.is_ge)
                    nc.vector.tensor_tensor(eq[:, h, 0:n, :], iota_ps[:, None, 0:tiles].to_broadcast([P, n, tiles]),
                                            hi[:, at, None].to_broadcast([P, n, tiles]),
                                            ALU.is_equal).then_inc(flags_ready, 1)
                    if not (first and s == 0):
                        dve.wait_ge(chain, base)
                    nc.vector.tensor_scalar(fresh_blk[:, h, 0:n], fresh[:, at], 0.0, None,
                                            ALU.add).then_inc(chain, 1)
                    if not (first and s == 0):
                        dve.wait_ge(evacuated, blk)
                    dve.wait_ge(gathered[s], k * (16 * STEPS) + 16 * n)
                    for t in range(n):
                        before_ps = run_ps(h, t - 1) if t else run_ps(1 - h, (sizes[s - 1] if s else STEPS) - 1)
                        dve.wait_ge(chain, base + (t + 1))
                        nc.vector.scalar_tensor_tensor(run_ps(h, t), before_ps, fresh_blk[:, h, t:t + 1],
                                                       rows[:, s * STEPS + t, :], ALU.add, ALU.max).then_inc(chain, 1)
            then(nc.vector.tensor_copy(before[:, :], before_i[:, 0:1]))
            then(nc.vector.tensor_scalar(lo_i[:, :], dst_f[:, :], dst_f[:, 0:1], None, ALU.is_equal))
            settled()
            then(nc.vector.reduce_sum(run[:, :], lo_i[:, :], AX.X))
            then(nc.vector.tensor_tensor(linked[:, :], before[:, :], dst_f[:, 0:1], ALU.is_equal))
            settled()
            then(nc.vector.tensor_scalar(linked_low[:, :], linked[:, :], 1.0, -LOW, ALU.subtract, ALU.mult))
            then(nc.vector.scalar_tensor_tensor(whole[:, :], run[:, :], float(cols), linked[:, :], ALU.is_equal, ALU.mult))
            then(nc.vector.tensor_scalar(mend_f[:, :], part_f[:, :], float(cols), -1.0, ALU.mult, ALU.add))
            settled()
            nc.vector.tensor_scalar(whole_diag[:, :], ident[:, :], whole[:, 0:1], None, ALU.mult).then_inc(whole_ready, 1)
            nc.vector.tensor_tensor(mend_idx[:, :], mend_f[:, :], run[:, :], ALU.add).then_inc(mend_idx_ready, 1)
            then(nc.vector.tensor_tensor(lo_i[:, 1:cols], dst_f[:, 1:cols], dst_f[:, 0:cols - 1], ALU.is_lt))
            then(nc.vector.tensor_tensor(drop[:, :], dst_f[:, 0:1], before[:, :], ALU.is_lt))
            settled()
            then(nc.vector.reduce_sum(drops[:, :], lo_i[:, 1:cols], AX.X))
            settled()
            nc.vector.tensor_tensor(drops[:, :], drops[:, :], drop[:, :], ALU.add).then_inc(drops_ready, 1)
            then(nc.vector.tensor_scalar(step_down[:, :], iota_f[:, :], part_f[:, 0:1], 1.0, ALU.subtract, ALU.is_equal))
            then(nc.vector.tensor_scalar(whole_low[:, 0:1], part_f[:, :], float(P - 1), None, ALU.is_equal))
            settled()
            then(nc.vector.tensor_tensor(step_down[:, :], ident[:, :], step_down[:, :], ALU.subtract))
            then(nc.vector.tensor_scalar(last_row[:, :], ones[:, :], whole_low[:, 0:1], None, ALU.mult))
            settled()

            blocks(0, True, FULL_TURN)
            with dve.Fori(1, turns) as k:
                blocks(k, False, FULL_TURN)
            blocks(turns, False, LAST_TURN)

            dve.wait_ge(whole_made, 1)
            then(nc.vector.tensor_scalar(whole_low[:, :], whole_ps, 1.0, -LOW, ALU.subtract, ALU.mult))
            dve.wait_ge(tailT_made, 1)
            then(nc.vector.tensor_copy(tails_T[:, :], tailT_ps))
            then(nc.vector.memset(carried_T[:, 0:1], 0.0))
            settled()
            nc.vector.tensor_tensor_scan(carried_T[:, 1:P + 1], whole_low[:, :], tails_T[:, :], LOW,
                                         ALU.add, ALU.max).then_inc(carried_ready, 1)
            dve.wait_ge(drops_made, 1)
            nc.vector.tensor_copy(disorder[:, :], drops_ps).then_inc(disorder_ready, 1)
            dve.wait_ge(count_done, 1)
            nc.vector.tensor_copy(counts[:, :], count_ps).then_inc(counts_ready, 1)
            dve.wait_ge(mend_in, 16)
            dve.wait_ge(carry_made, 1)
            nc.vector.scalar_tensor_tensor(mended[:, :], carry_ps, linked_low[:, 0:1], mend[:, :],
                                           ALU.add, ALU.max).then_inc(mended_ready, 1)
            dve.wait_ge(totals_made, 1)
            then(nc.vector.tensor_copy(ends[:, :], totals_ps))
            then(nc.vector.tensor_scalar(has_edges[:, :], degree_ps, 0.0, None, ALU.is_gt))
            settled()
            then(nc.vector.tensor_tensor_scan(upto[:, :], ones[:, 0:tiles], ends[:, :], 0.0, ALU.mult, ALU.add))
            settled()
            then(nc.vector.tensor_tensor(upto[:, :], upto[:, :], ends[:, :], ALU.subtract))
            settled()
            then(nc.vector.tensor_tensor(upto[:, :], upto[:, :], counts[:, :], ALU.add))
            settled()
            then(nc.vector.tensor_scalar(last_f[:, :], upto[:, :], float(-1 - zero_row), None, ALU.add))
            settled()
            then(nc.vector.tensor_tensor(last_f[:, :], last_f[:, :], has_edges[:, :], ALU.mult))
            settled()
            nc.vector.tensor_scalar(last_edge[:, :], last_f[:, :], float(zero_row), None, ALU.add).then_inc(last_ready, 1)

            then(nc.vector.tensor_tensor(dense[:, :, :], dense[:, :, :],
                                         has_edges[:, :, None].to_broadcast([P, tiles, D]), ALU.mult))
            settled()
            then(nc.vector.tensor_tensor(dense[:, :, :], dense[:, :, :], xs[:, :, :], ALU.add))
            settled()
            for g, (a, z) in enumerate(spans):
                dve.wait_ge(final_in[g], 16 * (z - a))
                nc.vector.tensor_tensor(rows[:, a:z, :], rows[:, a:z, :], dense[:, a:z, :],
                                        ALU.add).then_inc(final_ready, 1)


def kernel(**inputs):
    import numpy as np
    import concourse.bacc as bacc
    from concourse.bass_utils import run_bass_kernel_spmd as run

    nc = bacc.Bacc("TRN2", target_bir_lowering=False, num_devices=1)
    arrays, args = {}, []
    for name in ["x", "src", "dst", "L0_gnn_W", "L0_gnn_b"]:
        a = np.ascontiguousarray(inputs[name])
        arrays[f"in_{name}"] = a
        args.append(nc.dram_tensor(f"in_{name}", a.shape, mybir.dt.from_np(a.dtype), kind="ExternalInput").ap())
    args.append(nc.dram_tensor("out_x", inputs["x"].shape, F32, kind="ExternalOutput").ap())
    edgeconv(nc, *args)
    return run(nc, [arrays], core_ids=[0]).results[0]["out_x"]
```
